# Optimizing a Trainium2 kernel written in Bass

```python
import numpy as np
import jax
import jax.numpy as jnp

def _softmax(x, axis=-1):
    return jax.nn.softmax(x, axis=axis)

def _gelu(x):
    return jax.nn.gelu(x, approximate=True)

def _silu(x):
    return jax.nn.silu(x)

def _sigmoid(x):
    return jax.nn.sigmoid(x)

def _layernorm(x, axis=-1, eps=1e-05):
    m = jnp.mean(x, axis=axis, keepdims=True)
    v = jnp.var(x, axis=axis, keepdims=True)
    return (x - m) / jnp.sqrt(v + eps)

def _scatter_add(tgt, idx, src, axis=0):
    return tgt.at[idx].add(src)

def _segment_sum(src, seg, n):
    return jax.ops.segment_sum(src, seg, n)
kernel_name = 'mk_flamingo_gated_d1_seqx_r4_e22e0d'

def setup_inputs(seed: int=0):
    np.random.seed(seed)
    _w = jnp.asarray

    def _rec_inputs():
        import jax
        import jax.numpy as jnp
        _rk = jax.random.key(seed)
        x = 7.22e-05 + 1 * jax.random.normal(jax.random.fold_in(_rk, 1), (64, 128, 256), jnp.float32)
        _lenS = 128 - jax.random.randint(jax.random.fold_in(_rk, 7), (64,), 0, max(1, 128 // 4) + 1, jnp.int32)
        _lenS2 = 128 - jax.random.randint(jax.random.fold_in(_rk, 8), (64,), 0, max(1, 128 // 4) + 1, jnp.int32)
        _ctx_1024P = jax.random.normal(jax.random.fold_in(_rk, 11), (64, 16, 256), jnp.float32)
        _ctx_1024c = jax.random.dirichlet(jax.random.fold_in(_rk, 511), 0.3 * jnp.ones((16,), jnp.float32), (64, 128))
        _ctx_1024t = jnp.einsum('bsk,bkd->bsd', _ctx_1024c, _ctx_1024P)
        _ctx_1024t = _ctx_1024t * jax.lax.rsqrt(jnp.mean(jnp.square(_ctx_1024t)) + 1e-12) * 0.953939
        ctx_1024 = 4.13588e-05 + 0.999923 * (_ctx_1024t + 0.3 * jax.random.normal(jax.random.fold_in(_rk, 611), (64, 128, 256), jnp.float32))
        _g = jax.random.normal(jax.random.fold_in(_rk, 9001), (2, 1), jnp.float32)
        _g = jnp.sign(_g) * jnp.maximum(jnp.abs(_g), 1.0) + (_g == 0) * 1.0
        g_xattn = _g[0]
        g_ffn = _g[1]
        return (x, ctx_1024, g_xattn, g_ffn)
    x, ctx_1024, g_xattn, g_ffn = _rec_inputs()

    def _L0_xattn_setup():
        import jax, jax.numpy as jnp
        import numpy as np
        EMBED = 256
        HEADS = 16
        HEAD_DIM = EMBED // HEADS
        WINDOW = 256
        HALF = WINDOW // 2
        SCALE = HEAD_DIM ** (-0.5)
        B, T = (2, 1024)

        def _sliding_window_attn(q, k, v):
            Bq, H, Tq, D = q.shape
            Bk = HALF
            nb = Tq // Bk
            qb = q.reshape(Bq, H, nb, Bk, D)

            def ctx(x):
                xb = x.reshape(Bq, H, nb, Bk, D)
                prev = jnp.concatenate([jnp.zeros_like(xb[:, :, :1]), xb[:, :, :-1]], axis=2)
                return jnp.concatenate([prev, xb], axis=3)
            kc, vc = (ctx(k), ctx(v))
            scores = jnp.einsum('bhnrd,bhncd->bhnrc', qb, kc)
            r = jnp.arange(Bk)[:, None]
            c = jnp.arange(2 * Bk)[None, :]
            band = (c >= r) & (c <= r + Bk)
            b_idx = jnp.arange(nb)[:, None, None]
            valid = band[None] & ((b_idx > 0) | (c[None] >= Bk))
            neg_inf = jnp.finfo(jnp.float32).min
            scores = jnp.where(valid[None, None], scores.astype(jnp.float32), neg_inf)
            attn = jax.nn.softmax(scores, axis=-1).astype(q.dtype)
            out = jnp.einsum('bhnrc,bhncd->bhnrd', attn, vc)
            return out.reshape(Bq, H, Tq, D)
        key = jax.random.key(seed)
        ks = jax.random.split(key, 11)
        f = jnp.float32
        return {'query': jax.random.normal(ks[0], (B, T, EMBED), f), 'key': jax.random.normal(ks[1], (B, T, EMBED), f), 'value': jax.random.normal(ks[2], (B, T, EMBED), f), 'wq': jax.random.normal(ks[3], (EMBED, EMBED), f) * 0.02, 'bq': jax.random.normal(ks[4], (EMBED,), f) * 0.02, 'wk': jax.random.normal(ks[5], (EMBED, EMBED), f) * 0.02, 'bk': jax.random.normal(ks[6], (EMBED,), f) * 0.02, 'wv': jax.random.normal(ks[7], (EMBED, EMBED), f) * 0.02, 'bv': jax.random.normal(ks[8], (EMBED,), f) * 0.02, 'wo': jax.random.normal(ks[9], (EMBED, EMBED), f) * 0.02, 'bo': jax.random.normal(ks[10], (EMBED,), f) * 0.02}
    _L0_xattn_all = _L0_xattn_setup()
    _L0_xattn_in = {k: v for k, v in _L0_xattn_all.items() if k in ('wq', 'bq', 'wk', 'bk', 'wv', 'bv', 'wo', 'bo')}
    del _L0_xattn_all

    def _L0_ffn_setup():
        import jax, jax.numpy as jnp
        import numpy as np
        HIDDEN = 256
        NUM_EXPERTS = 8
        BATCH, SEQ = (4, 1024)
        key = jax.random.key(seed)
        ks = jax.random.split(key, 6)
        s = 1.0 / np.sqrt(HIDDEN)
        tokens = jax.random.normal(ks[0], (BATCH, SEQ, HIDDEN), dtype=jnp.float32)
        gate_w = jax.random.uniform(ks[1], (NUM_EXPERTS, HIDDEN), jnp.float32, -s, s)
        expert_w = jax.random.uniform(ks[2], (NUM_EXPERTS, HIDDEN, HIDDEN), jnp.float32, -s, s)
        expert_b = jax.random.uniform(ks[3], (NUM_EXPERTS, HIDDEN), jnp.float32, -s, s)
        combine_w = jax.random.uniform(ks[4], (HIDDEN, HIDDEN), jnp.float32, -s, s)
        return {'tokens': tokens, 'gate_w': gate_w, 'expert_w': expert_w, 'expert_b': expert_b, 'combine_w': combine_w}
    _L0_ffn_all = _L0_ffn_setup()
    _L0_ffn_in = {k: v for k, v in _L0_ffn_all.items() if k in ('gate_w', 'expert_w', 'expert_b', 'combine_w')}
    del _L0_ffn_all
    return {'x': x, 'ctx_1024': ctx_1024, 'g_xattn': g_xattn, 'g_ffn': g_ffn, 'L0_xattn_wq': _L0_xattn_in['wq'], 'L0_xattn_bq': _L0_xattn_in['bq'], 'L0_xattn_wk': _L0_xattn_in['wk'], 'L0_xattn_bk': _L0_xattn_in['bk'], 'L0_xattn_wv': _L0_xattn_in['wv'], 'L0_xattn_bv': _L0_xattn_in['bv'], 'L0_xattn_wo': _L0_xattn_in['wo'], 'L0_xattn_bo': _L0_xattn_in['bo'], 'L0_ffn_gate_w': _L0_ffn_in['gate_w'], 'L0_ffn_expert_w': _L0_ffn_in['expert_w'], 'L0_ffn_expert_b': _L0_ffn_in['expert_b'], 'L0_ffn_combine_w': _L0_ffn_in['combine_w']}

def reference(x, ctx_1024, g_xattn, g_ffn, L0_xattn_wq, L0_xattn_bq, L0_xattn_wk, L0_xattn_bk, L0_xattn_wv, L0_xattn_bv, L0_xattn_wo, L0_xattn_bo, L0_ffn_gate_w, L0_ffn_expert_w, L0_ffn_expert_b, L0_ffn_combine_w):
    import jax
    import jax.numpy as jnp

    def _L0_xattn_ref(query, key, value, wq, bq, wk, bk, wv, bv, wo, bo):
        import jax, jax.numpy as jnp
        import numpy as np
        EMBED = 256
        HEADS = 16
        HEAD_DIM = EMBED // HEADS
        WINDOW = 256
        HALF = WINDOW // 2
        SCALE = HEAD_DIM ** (-0.5)
        B, T = (2, 1024)

        def _sliding_window_attn(q, k, v):
            Bq, H, Tq, D = q.shape
            Bk = HALF
            nb = Tq // Bk
            qb = q.reshape(Bq, H, nb, Bk, D)

            def ctx(x):
                xb = x.reshape(Bq, H, nb, Bk, D)
                prev = jnp.concatenate([jnp.zeros_like(xb[:, :, :1]), xb[:, :, :-1]], axis=2)
                return jnp.concatenate([prev, xb], axis=3)
            kc, vc = (ctx(k), ctx(v))
            scores = jnp.einsum('bhnrd,bhncd->bhnrc', qb, kc)
            r = jnp.arange(Bk)[:, None]
            c = jnp.arange(2 * Bk)[None, :]
            band = (c >= r) & (c <= r + Bk)
            b_idx = jnp.arange(nb)[:, None, None]
            valid = band[None] & ((b_idx > 0) | (c[None] >= Bk))
            neg_inf = jnp.finfo(jnp.float32).min
            scores = jnp.where(valid[None, None], scores.astype(jnp.float32), neg_inf)
            attn = jax.nn.softmax(scores, axis=-1).astype(q.dtype)
            out = jnp.einsum('bhnrc,bhncd->bhnrd', attn, vc)
            return out.reshape(Bq, H, Tq, D)
        Bq, Tq, C = query.shape
        split = lambda x: x.reshape(Bq, Tq, HEADS, HEAD_DIM).transpose(0, 2, 1, 3)
        q = split(jnp.einsum('btc,oc->bto', query, wq) + bq) * SCALE
        k = split(jnp.einsum('btc,oc->bto', key, wk) + bk)
        v = split(jnp.einsum('btc,oc->bto', value, wv) + bv)
        o = _sliding_window_attn(q, k, v)
        o = o.transpose(0, 2, 1, 3).reshape(Bq, Tq, C)
        return jnp.einsum('btc,oc->bto', o, wo) + bo

    def _L0_ffn_ref(tokens, gate_w, expert_w, expert_b, combine_w):
        import jax, jax.numpy as jnp
        import numpy as np
        HIDDEN = 256
        NUM_EXPERTS = 8
        BATCH, SEQ = (4, 1024)
        B, S, H = tokens.shape
        logits = jnp.einsum('bsh,eh->bse', tokens, gate_w)
        probs = jax.nn.softmax(logits, axis=-1)
        top2_w, top2_idx = jax.lax.top_k(probs, 2)
        flat = tokens.reshape(B * S, H)
        flat_idx = top2_idx.reshape(B * S, 2)
        flat_w = top2_w.reshape(B * S, 2)
        expert_out = jax.nn.silu(jnp.einsum('nh,edh->ned', flat, expert_w) + expert_b[None, :, :])
        gathered = jnp.take_along_axis(expert_out, flat_idx[:, :, None], axis=1)
        mixed = jnp.sum(gathered * flat_w[:, :, None], axis=1)
        out = jnp.einsum('bsh,dh->bsd', mixed.reshape(B, S, H), combine_w)
        return out
    x = x + jnp.tanh(g_xattn[0]) * _L0_xattn_ref(_layernorm(x, axis=-1), ctx_1024, ctx_1024, L0_xattn_wq, L0_xattn_bq, L0_xattn_wk, L0_xattn_bk, L0_xattn_wv, L0_xattn_bv, L0_xattn_wo, L0_xattn_bo)
    x = x + jnp.tanh(g_ffn[0]) * _L0_ffn_ref(_layernorm(x, axis=-1), L0_ffn_gate_w, L0_ffn_expert_w, L0_ffn_expert_b, L0_ffn_combine_w)
    return x

_drawn_inputs = setup_inputs


def setup_inputs(seed=0):
    import zlib

    import numpy as np

    out = dict(_drawn_inputs(seed))
    spreads = {}
    factors = {'L0_xattn_wq': 8.0,
     'L0_xattn_bq': 54.06,
     'L0_xattn_wk': 8.0,
     'L0_xattn_bk': 64.0,
     'L0_xattn_bv': 8.0,
     'L0_xattn_bo': 3.506,
     'L0_ffn_expert_b': 8.0}
    for name, (base, spread) in spreads.items():
        noise = np.random.default_rng([zlib.crc32(name.encode()), seed]).standard_normal(out[name].shape)
        drawn = base * np.exp(spread * noise) if base else spread * noise
        out[name] = jnp.asarray(drawn.astype(out[name].dtype))
    for name, factor in factors.items():
        out[name] = (out[name] * factor).astype(out[name].dtype)
    return out
```

```python
from contextlib import ExitStack

import concourse.bass as bass
from concourse import mybir

P = 128
ALU = mybir.AluOpType
ACT = mybir.ActivationFunctionType
AX_X = mybir.AxisListType.X
F32 = mybir.dt.float32
F32R = mybir.dt.float32r
BF16 = mybir.dt.bfloat16
FP16 = mybir.dt.float16

C_IDENT = 0
C_CAUSAL = 128
C_PARITY = 256
C_LOWER = 258
C_COLS = 258 + 64


def flamingo_block(
    nc: bass.Bass,
    x: bass.AP,
    ctx_1024: bass.AP,
    g_xattn: bass.AP,
    g_ffn: bass.AP,
    L0_xattn_wq: bass.AP,
    L0_xattn_bq: bass.AP,
    L0_xattn_wk: bass.AP,
    L0_xattn_bk: bass.AP,
    L0_xattn_wv: bass.AP,
    L0_xattn_bv: bass.AP,
    L0_xattn_wo: bass.AP,
    L0_xattn_bo: bass.AP,
    L0_ffn_gate_w: bass.AP,
    L0_ffn_expert_w: bass.AP,
    L0_ffn_expert_b: bass.AP,
    L0_ffn_combine_w: bass.AP,
    consts: bass.AP,
    out: bass.AP,
):
    NSEQ, T, C = x.shape
    NPAIR = NSEQ // 2
    KC = C // P
    HD = 16
    H = C // HD
    NE = L0_ffn_expert_w.shape[0]
    VC = 3 * HD + 1
    SU = 8
    EU = 8
    SCALE = float(HD) ** -0.5
    EPS = 1e-5
    assert T == P and C == 2 * P and H == 16 and NE == 8

    with ExitStack() as ctx:
        def sb(name, shape, dt=F32):
            return ctx.enter_context(nc.sbuf_tensor(name, shape, dt))

        def sem(name):
            return ctx.enter_context(nc.semaphore(name))

        cst = sb("cst", [P, C_COLS])
        ident = cst[:, C_IDENT:C_IDENT + P]
        parity = [cst[:, C_PARITY + j:C_PARITY + j + 1] for j in range(2)]
        ident_bf = sb("ident_bf", [P, P], BF16)
        causal_bf = sb("causal_bf", [P, 4, P], BF16)
        half_neg = sb("half_neg", [P, 2])
        bias_sel = sb("bias_sel", [P, P], BF16)
        ebias = sb("ebias", [P, NE * C], BF16)
        eb_nat = sb("eb_nat", [16, P])
        eb_rest = sb("eb_rest", [16, 2, P])
        eb_part = sb("eb_part", [16, 3, P], BF16)
        gates = sb("gates", [P, 4])
        g_raw = sb("g_raw", [P, 2])
        bq_col = sb("bq_col", [P, KC])
        bk_col = sb("bk_col", [P, KC])
        bv_row = sb("bv_row", [P, C])
        bo_row = sb("bo_row", [P, C])
        w_nat = sb("w_nat", [P, 6 + NE, KC, C])
        w_hi = sb("w_hi", [P, 5, KC, C], F32R)
        w_lo = sb("w_lo", [P, 5, KC, C], F32R)
        gw_hi = sb("gw_hi", [P, KC, P], F32R)
        gw_lo = sb("gw_lo", [P, KC, P], F32R)
        ew_hi = sb("ew_hi", [P, KC, NE, C], F32R)
        ew_lo = sb("ew_lo", [P, KC, NE, C], F32R)

        x_in = sb("x_in", [P, 2, C])
        c_in = sb("c_in", [P, 2, C])
        x_res = sb("x_res", [P, 2, C])
        xb = sb("xb", [P, 2, C])
        st1 = sb("st1", [P, 2, 6])
        mv1 = sb("mv1", [P, 2, 2])
        ve1 = sb("ve1", [P, 2])
        rstd1 = sb("rstd1", [P, 2])
        xn = sb("xn", [P, 2, C])
        xT_hi = sb("xT_hi", [P, KC, 2, P], F32R)
        xT_lo = sb("xT_lo", [P, KC, 2, P], F32R)
        cT_hi = sb("cT_hi", [P, KC, 2, P], F32R)
        cT_lo = sb("cT_lo", [P, KC, 2, P], F32R)
        q32 = sb("q32", [P, KC, 2 * P])
        k32 = sb("k32", [P, KC, 2 * P])
        q_hi = sb("q_hi", [P, KC, 2, P], F32R)
        q_lo = sb("q_lo", [P, KC, 2, P], F32R)
        k_hi = sb("k_hi", [P, KC, 2, 2, P], F32R)
        k_lo = sb("k_lo", [P, KC, 2, 2, P], F32R)
        v32 = sb("v32", [P, 2, C])
        v_rest = sb("v_rest", [P, 2, C])
        v_part = sb("v_part", [P, 2, H, VC], BF16)
        neg_max = sb("neg_max", [P, SU, 4])
        e_q = sb("e_q", [P, 4, 4, P])
        e_hi = sb("e_hi", [P, 2, 4, P], FP16)
        e_lo = sb("e_lo", [P, 2, 4, P], FP16)
        inv_sum = sb("inv_sum", [P, 2, 4])
        o_sum = sb("o_sum", [P, 2, 4, HD])
        o_n = sb("o_n", [P, 2, 2, 2, 4, HD])
        oT_hi = sb("oT_hi", [P, KC, 2, P], F32R)
        oT_lo = sb("oT_lo", [P, KC, 2, P], F32R)
        x1 = sb("x1", [P, 2, C])
        x1_kept = sb("x1_kept", [P, 2, C])
        st2 = sb("st2", [P, 2, 6])
        mv2 = sb("mv2", [P, 2, 2])
        ve2 = sb("ve2", [P, 2])
        rstd2 = sb("rstd2", [P, 2])
        xn2 = sb("xn2", [P, 2, C])
        x2T_hi = sb("x2T_hi", [P, KC, 2, P], F32R)
        x2T_lo = sb("x2T_lo", [P, KC, 2, P], F32R)
        lgT = sb("lgT", [P, 2, P])
        r_max = sb("r_max", [P, 2])
        r_sub = sb("r_sub", [P, 2, NE])
        r_exp = sb("r_exp", [P, 2, NE])
        r_sum = sb("r_sum", [P, 2])
        r_inv = sb("r_inv", [P, 2])
        prob = sb("prob", [P, 2, NE])
        cmp_gt = sb("cmp_gt", [P, 2, NE, NE])
        cmp_eq = sb("cmp_eq", [P, 2, NE, NE])
        rank = sb("rank", [P, 2, NE])
        w_tok = sb("w_tok", [P, 2, NE])
        act_e = sb("act_e", [P, 2, 2, C])
        mix = sb("mix", [P, 2, C])
        mT_hi = sb("mT_hi", [P, KC, 2, P], F32R)
        mT_lo = sb("mT_lo", [P, KC, 2, P], F32R)
        y = sb("y", [P, 2, C])

        banks = [ctx.enter_context(nc.psum_tensor(f"bank{i}", [P, 512], F32)) for i in range(8)]
        S = [banks[0], banks[1]]
        TB = banks[2]
        OB = banks[3]
        E = [banks[4], banks[5]]
        G0, G1 = banks[6], banks[7]

        def quad(b):
            return b[:, :].rearrange("p (a s t) -> p a s t", a=2, s=2)

        ld_first = sem("ld_first")
        ld_rest = sem("ld_rest")
        ld_experts = sem("ld_experts")
        w_cleared = sem("w_cleared")
        gates_ready = sem("gates_ready")
        w_transposed = sem("w_transposed")
        w_hi_ready = sem("w_hi_ready")
        w_lo_ready = sem("w_lo_ready")
        consts_ready = sem("consts_ready")
        pool_setup = sem("pool_setup")
        eb_step = sem("eb_step")
        ebias_ready = sem("ebias_ready")

        x_loaded = sem("x_loaded")
        c_loaded = sem("c_loaded")
        res_loaded = sem("res_loaded")
        y_stored = sem("y_stored")
        ln1_step = sem("ln1_step")
        rstd1_ready = sem("rstd1_ready")
        xn_ready = sem("xn_ready")
        xt_done = sem("xt_done")
        xTh_ready = sem("xTh_ready")
        xTl_ready = sem("xTl_ready")
        ct_done = sem("ct_done")
        cTh_ready = sem("cTh_ready")
        cTl_ready = sem("cTl_ready")
        q_done = sem("q_done")
        q32_ready = sem("q32_ready")
        qh_ready = sem("qh_ready")
        ql_ready = sem("ql_ready")
        k_done = sem("k_done")
        k32_ready = sem("k32_ready")
        kh_ready = sem("kh_ready")
        kl_ready = sem("kl_ready")
        v_done = sem("v_done")
        v32_ready = sem("v32_ready")
        v_split = sem("v_split")
        s_done = sem("s_done")
        max_ready = sem("max_ready")
        exp_ready = sem("exp_ready")
        t_done = sem("t_done")
        eh_ready = sem("eh_ready")
        el_ready = sem("el_ready")
        pv_done = sem("pv_done")
        norm_step = sem("norm_step")
        norm_ready = sem("norm_ready")
        ot_done = sem("ot_done")
        oTh_ready = sem("oTh_ready")
        oTl_ready = sem("oTl_ready")
        p_done = sem("p_done")
        xb_ready = sem("xb_ready")
        x1_ready = sem("x1_ready")
        x1_copied = sem("x1_copied")
        ln2_step = sem("ln2_step")
        rstd2_ready = sem("rstd2_ready")
        xn2_ready = sem("xn2_ready")
        x2t_done = sem("x2t_done")
        x2h_ready = sem("x2h_ready")
        x2l_ready = sem("x2l_ready")
        gl_done = sem("gl_done")
        lgT_ready = sem("lgT_ready")
        gt_done = sem("gt_done")
        rmax_ready = sem("rmax_ready")
        rsub_ready = sem("rsub_ready")
        rexp_ready = sem("rexp_ready")
        prob_step = sem("prob_step")
        cmp_ready = sem("cmp_ready")
        cmp_step = sem("cmp_step")
        rank_step = sem("rank_step")
        e_done = sem("e_done")
        silu_ready = sem("silu_ready")
        acc_step = sem("acc_step")
        mt_done = sem("mt_done")
        mTh_ready = sem("mTh_ready")
        mTl_ready = sem("mTl_ready")
        comb_done = sem("comb_done")
        y_ready = sem("y_ready")

        def wait(eng, s, value):
            if not (isinstance(value, int) and value <= 0):
                eng.wait_ge(s, value)

        def wait_alone(eng, s, value):
            wait(eng, s, value)
            eng.nop(nofuse=True)

        def stages(i):
            if not isinstance(i, int):
                return True, True, True, True, True
            return tuple(0 <= i - d < NPAIR for d in range(5))

        FILL = 5

        def run_steps(eng, step):
            for i in range(FILL):
                step(i)
            with eng.Fori(FILL, NPAIR) as i:
                step(i)
            for i in range(NPAIR, NPAIR + 4):
                step(i)

        attn_w = [L0_xattn_wq, L0_xattn_wk, L0_xattn_wv, L0_xattn_wo, L0_ffn_combine_w]
        scale_of = [3, 0, 0, 1, 2]
        WQ, WK, WV, WO, WC = range(5)
        x_pairs = x.rearrange("(i s) p c -> i p s c", s=2)
        c_pairs = ctx_1024.rearrange("(i s) p c -> i p s c", s=2)
        out_pairs = out.rearrange("(i s) p c -> i p s c", s=2)
        N_FIRST = 16 * (2 + 2 + len(attn_w) + 4)
        PREP = 5 + 1 + NE

        block = ctx.enter_context(nc.Block())

        @block.sync
        def _(sp):
            sp.dma_start(cst[:], consts).then_inc(ld_first, 16)
            for j, w in enumerate(attn_w):
                sp.dma_start(w_nat[:, j], w.rearrange("(a p) c -> p a c", p=P)).then_inc(ld_first, 16)
            sp.wait_ge(w_cleared, 1)
            sp.dma_start(w_nat[0:NE, 5, 0, :], L0_ffn_gate_w).then_inc(ld_first, 16)
            for j, g in enumerate((g_xattn, g_ffn)):
                sp.dma_start(g_raw[:, j:j + 1], g.rearrange("(o n) -> o n", o=1).broadcast_to([P, 1])
                             ).then_inc(ld_first, 16)
            for col, b in ((bq_col, L0_xattn_bq), (bk_col, L0_xattn_bk)):
                sp.dma_start(col[:], b.rearrange("(a p) -> p a", p=P), allow_slow_non_contiguous=True).then_inc(ld_first, 16)
            for row, b in ((bv_row, L0_xattn_bv), (bo_row, L0_xattn_bo)):
                sp.dma_start(row[:], b.rearrange("(o n) -> o n", o=1).broadcast_to([P, C])
                             ).then_inc(ld_first, 16)
            sp.dma_start(eb_nat[:], L0_ffn_expert_b.rearrange("e (h c) -> (e h) c", c=P)).then_inc(ld_rest, 16)

            def step(i):
                front, _, back1, _, back3 = stages(i)
                if back1:
                    wait(sp, xb_ready, i - 2)
                    sp.dma_start(x_res[:], x_pairs[i - 2]).then_inc(res_loaded, 16)
                if front:
                    wait(sp, xn_ready, i)
                    sp.dma_start(x_in[:], x_pairs[i]).then_inc(x_loaded, 16)
                    wait(sp, ct_done, i)
                    sp.dma_start(c_in[:], c_pairs[i]).then_inc(c_loaded, 16)
                if isinstance(i, int) and i == 0:
                    for e in range(NE):
                        sp.dma_start(w_nat[:, 6 + e], L0_ffn_expert_w[e].rearrange("(a p) c -> p a c", p=P)
                                     ).then_inc(ld_experts, 16)
                    sp.wait_ge(eb_step, 5)
                    sp.wait_ge(pool_setup, 2)
                    for k in range(3):
                        sp.dma_start(ebias[k:k + 1, :].rearrange("o (h c) -> o h c", c=P),
                                     eb_part[:, k, :]).then_inc(ebias_ready, 16)
                if back3:
                    wait(sp, y_ready, i - 3)
                    sp.dma_start(out_pairs[i - 4], y[:]).then_inc(y_stored, 16)

            run_steps(sp, step)
            sp.wait_ge(y_stored, 16 * NPAIR)

        @block.tensor
        def _(pe):
            mm = nc.tensor.matmul

            def transpose4(bank, src, done):
                for s in range(2):
                    for a in range(KC):
                        last = nc.tensor.transpose(quad(bank)[:, a, s, :], src[:, s, a * P:(a + 1) * P], ident)
                last.then_inc(done, 1)

            def project_T(bank, w, hi, lo, done):
                for a in range(KC):
                    terms = [(l[:, w, kc, a * P:(a + 1) * P], r[:, kc, :, :])
                             for l, r in ((w_hi, hi), (w_hi, lo), (w_lo, hi)) for kc in range(KC)]
                    for n, (l, r) in enumerate(terms):
                        last = mm(bank[:, a * 256:(a + 1) * 256], l, r, start=n == 0, stop=n == len(terms) - 1)
                last.then_inc(done, 1)

            def project(bank, w, hi, lo, done):
                for s in range(2):
                    terms = [(l[:, kc, s, :], r[:, w, kc, :])
                             for l, r in ((hi, w_hi), (hi, w_lo), (lo, w_hi)) for kc in range(KC)]
                    for n, (l, r) in enumerate(terms):
                        last = mm(bank[:, s * 256:(s + 1) * 256], l, r, start=n == 0, stop=n == len(terms) - 1)
                last.then_inc(done, 1)

            def scores(p, u):
                s, g = divmod(u, 4)
                rows = slice(32 * g, 32 * g + 32)
                bank = S[u % 2]
                if u == 0:
                    pe.wait_ge(ql_ready, p + 1)
                    pe.wait_ge(kl_ready, p + 1)
                wait(pe, exp_ready, 8 * p + u - 1)
                mm(bank[:, :], ident_bf[:], causal_bf[:], start=True, stop=False, skip_group_check=True)
                for a in range(KC):
                    for n, (l, r) in enumerate(((q_hi, k_hi), (q_lo, k_hi), (q_hi, k_lo))):
                        last = mm(bank[:, a * 256:(a + 1) * 256], l[rows, a, s, :],
                                  r[rows, a, s, :, :], start=False, stop=n == 2, skip_group_check=True)
                last.then_inc(s_done, 1)

            def transposed_exp(p, u):
                pe.wait_ge(exp_ready, 8 * p + u + 1)
                wait(pe, el_ready, 8 * p + u)
                for j in range(4):
                    last = nc.tensor.transpose(TB[:, j * P:(j + 1) * P], e_q[:, u % 4, j, :], ident)
                last.then_inc(t_done, 1)

            def times_v(p, u):
                s, g = divmod(u, 4)
                if u == 0:
                    pe.wait_ge(v_split, 5 * p + 5)
                pe.wait_ge(el_ready, 8 * p + u + 1)
                if u % 2 == 0:
                    wait(pe, norm_ready, 4 * p + u // 2)
                for j in range(4):
                    a, odd = divmod(j, 2)
                    c0 = (4 * a + 2 * (u % 2) + odd) * VC
                    v = v_part[:, s, 8 * a + 2 * g + odd, :]
                    mm(OB[:, c0:c0 + VC], e_hi[:, u % 2, j, :], v, start=True, stop=False)
                    last = mm(OB[:, c0:c0 + VC], e_lo[:, u % 2, j, :], v, start=False, stop=True)
                last.then_inc(pv_done, 1)

            def expert_pair(p, e):
                s, f = divmod(e, 4)
                bank = E[e % 2]
                if e == 0:
                    pe.wait_ge(x2l_ready, p + 1)
                wait(pe, silu_ready, 8 * p + e - 1)
                mm(bank[:, :], bias_sel[:], ebias[:, f * 512:(f + 1) * 512], start=True, stop=False)
                terms = [(l[:, kc, s, :], r[:, kc, 2 * f:2 * f + 2, :])
                         for kc in range(KC) for l, r in ((x2T_hi, ew_hi), (x2T_hi, ew_lo), (x2T_lo, ew_hi))]
                for n, (l, r) in enumerate(terms):
                    last = mm(bank[:, :], l, r, start=False, stop=n == len(terms) - 1)
                last.then_inc(e_done, 1)

            def prepare(m):
                bank = banks[m % 8]
                if m >= 8:
                    pe.wait_ge(w_lo_ready, m - 7)
                for a in range(KC):
                    for kc in range(KC):
                        if m == 5 and a == 1:
                            continue
                        o = bank[:, kc * C + a * P:kc * C + (a + 1) * P]
                        last = nc.tensor.transpose(o, w_nat[:, m, a, kc * P:(kc + 1) * P], ident)
                last.then_inc(w_transposed, 1)

            pe.wait_ge(ld_first, N_FIRST)
            for m in range(6):
                prepare(m)
            pe.wait_ge(ld_experts, 16 * NE)
            for m in range(6, PREP):
                prepare(m)
            pe.wait_ge(w_lo_ready, PREP)
            pe.wait_ge(consts_ready, 2)
            pe.wait_ge(pool_setup, 3)
            pe.wait_ge(ebias_ready, 48)

            def step(i):
                front, attend, back1, back2, back3 = stages(i)
                fi = isinstance(i, int)
                if not fi or 1 <= i <= NPAIR:
                    pe.wait_ge(k32_ready, i)
                    pe.wait_ge(v32_ready, i)
                elif i > NPAIR:
                    wait(pe, x1_ready, min(i - 2, NPAIR))
                    wait(pe, rsub_ready, min(i - 3, NPAIR))
                    wait(pe, y_ready, min(i - 4, NPAIR))
                    wait(pe, mTl_ready, min(i - 4, NPAIR))
                if back2:
                    pe.wait_ge(xn2_ready, i - 2)
                    transpose4(G0, xn2, x2t_done)
                if attend:
                    scores(i - 1, 0)
                if back3:
                    pe.wait_ge(acc_step, 16 * (i - 3))
                    transpose4(G1, mix, mt_done)
                if attend:
                    scores(i - 1, 1)
                if back2:
                    pe.wait_ge(x2l_ready, i - 2)
                    for n in range(3):
                        l, r = ((gw_hi, x2T_hi), (gw_hi, x2T_lo), (gw_lo, x2T_hi))[n]
                        for kc in range(KC):
                            last = mm(G0[:, 0:256], l[:, kc, :], r[:, kc, :, :],
                                      start=n == 0 and kc == 0, stop=n == 2 and kc == 1)
                    last.then_inc(gl_done, 1)
                if back1:
                    pe.wait_ge(norm_ready, 4 * (i - 1))
                    if back3:
                        pe.wait_ge(mTl_ready, i - 3)
                    transpose4(G1, o_n[:].rearrange("p s a b h d -> p s (a b h d)"), ot_done)
                if attend:
                    transposed_exp(i - 1, 0)
                if back3:
                    pe.wait_ge(mTl_ready, i - 3)
                    if back2:
                        pe.wait_ge(lgT_ready, i - 2)
                    project(G0, WC, mT_hi, mT_lo, comb_done)
                if attend:
                    scores(i - 1, 2)
                if back2:
                    pe.wait_ge(lgT_ready, i - 2)
                    if back1:
                        pe.wait_ge(oTl_ready, i - 1)
                    elif back3:
                        pe.wait_ge(mTl_ready, i - 3)
                    for s in range(2):
                        last = nc.tensor.transpose(G1[:, s * P:(s + 1) * P], lgT[:, s, :], ident)
                    last.then_inc(gt_done, 1)
                if attend:
                    transposed_exp(i - 1, 1)
                    times_v(i - 1, 0)
                if back1:
                    pe.wait_ge(oTl_ready, i - 1)
                    if back3:
                        pe.wait_ge(y_ready, i - 3)
                    elif back2:
                        pe.wait_ge(lgT_ready, i - 2)
                    project(G0, WO, oT_hi, oT_lo, p_done)
                if attend:
                    scores(i - 1, 3)
                    times_v(i - 1, 1)
                    transposed_exp(i - 1, 2)
                if front:
                    pe.wait_ge(xn_ready, i + 1)
                    if back2:
                        pe.wait_ge(rsub_ready, i - 2)
                    elif back1:
                        pe.wait_ge(oTl_ready, i - 1)
                    transpose4(G1, xn, xt_done)
                if attend:
                    scores(i - 1, 4)
                    times_v(i - 1, 2)
                    transposed_exp(i - 1, 3)
                if front:
                    pe.wait_ge(c_loaded, 16 * (i + 1))
                    if back1:
                        pe.wait_ge(x1_ready, i - 1)
                    transpose4(G0, c_in, ct_done)
                if attend:
                    scores(i - 1, 5)
                    times_v(i - 1, 3)
                    transposed_exp(i - 1, 4)
                    scores(i - 1, 6)
                    times_v(i - 1, 4)
                    transposed_exp(i - 1, 5)
                    scores(i - 1, 7)
                if front:
                    pe.wait_ge(xTl_ready, i + 1)
                    project_T(G1, WQ, xT_hi, xT_lo, q_done)
                if back2:
                    expert_pair(i - 3, 0)
                if front:
                    pe.wait_ge(cTl_ready, i + 1)
                    project_T(G0, WK, cT_hi, cT_lo, k_done)
                if back2:
                    expert_pair(i - 3, 1)
                if attend:
                    times_v(i - 1, 5)
                    transposed_exp(i - 1, 6)
                if back2:
                    expert_pair(i - 3, 2)
                if front:
                    pe.wait_ge(q32_ready, i + 1)
                    project(G1, WV, cT_hi, cT_lo, v_done)
                if back2:
                    expert_pair(i - 3, 3)
                if attend:
                    times_v(i - 1, 6)
                    transposed_exp(i - 1, 7)
                if back2:
                    expert_pair(i - 3, 4)
                if attend:
                    times_v(i - 1, 7)
                if back2:
                    for e in range(5, EU):
                        expert_pair(i - 3, e)

            run_steps(pe, step)

        @block.scalar
        def _(act):
            def hi_of(bank, dst, done, ready):
                nc.scalar.activation(dst[:, :, :, :], quad(bank), ACT.Copy).then_inc(ready, 1)

            act.wait_ge(ld_first, N_FIRST)
            nc.scalar.activation(gates[:, 1:3], g_raw[:], ACT.Tanh).then_inc(gates_ready, 1)
            act.wait_ge(gates_ready, 2)
            for m in range(PREP):
                act.wait_ge(w_transposed, m + 1)
                bank = banks[m % 8]
                if m < 5:
                    src, dst, g = bank[:, :].rearrange("p (k c) -> p k c", k=KC), w_hi[:, m], scale_of[m]
                elif m == 5:
                    src, dst, g = bank[:, :].rearrange("p (k c) -> p k c", k=KC)[:, :, 0:P], gw_hi[:], 0
                else:
                    src, dst, g = bank[:, :].rearrange("p (k c) -> p k c", k=KC), ew_hi[:, :, m - 6, :], 0
                nc.scalar.activation(dst, src, ACT.Copy, scale=gates[:, g:g + 1]).then_inc(w_hi_ready, 1)

            def exps(p, u):
                act.wait_ge(max_ready, 8 * p + u + 1)
                wait(act, t_done, 8 * p + u - 3)
                for j in range(4):
                    last = nc.scalar.activation(e_q[:, u % 4, j, :], S[u % 2][:, j * P:(j + 1) * P], ACT.Exp,
                                                bias=neg_max[:, u, j:j + 1])
                last.then_inc(exp_ready, 1)

            def exp_hi(p, u):
                act.wait_ge(t_done, 8 * p + u + 1)
                wait(act, pv_done, 8 * p + u - 1)
                nc.scalar.activation(e_hi[:, u % 2, :, :], TB[:, :].rearrange("p (j t) -> p j t", j=4),
                                     ACT.Copy).then_inc(eh_ready, 1)

            def silu(p, e):
                act.wait_ge(e_done, 8 * p + e + 1)
                wait(act, acc_step, 2 * (8 * p + e - 1))
                nc.scalar.activation(act_e[:, e % 2, :, :], E[e % 2][:, :].rearrange("p (f c) -> p f c", f=2),
                                     ACT.Silu).then_inc(silu_ready, 1)

            def step(i):
                front, attend, back1, back2, back3 = stages(i)
                if back2:
                    act.wait_ge(x2t_done, i - 2)
                    wait(act, e_done, 8 * (i - 3))
                    hi_of(G0, x2T_hi, x2t_done, x2h_ready)
                if attend:
                    exps(i - 1, 0)
                if back3:
                    act.wait_ge(mt_done, i - 3)
                    wait(act, comb_done, i - 4)
                    hi_of(G1, mT_hi, mt_done, mTh_ready)
                if attend:
                    exps(i - 1, 1)
                if back2:
                    act.wait_ge(gl_done, i - 2)
                    wait(act, gt_done, i - 3)
                    nc.scalar.activation(lgT[:], G0[:, 0:256].rearrange("p (s t) -> p s t", s=2),
                                         ACT.Copy).then_inc(lgT_ready, 1)
                if back1:
                    act.wait_ge(ot_done, i - 1)
                    wait(act, p_done, i - 2)
                    hi_of(G1, oT_hi, ot_done, oTh_ready)
                if attend:
                    exp_hi(i - 1, 0)
                    exps(i - 1, 2)
                if back2:
                    act.wait_ge(rsub_ready, i - 2)
                    nc.scalar.activation(r_exp[:], r_sub[:], ACT.Exp).then_inc(rexp_ready, 1)
                if attend:
                    exp_hi(i - 1, 1)
                    exps(i - 1, 3)
                    exp_hi(i - 1, 2)
                if front:
                    act.wait_ge(xt_done, i + 1)
                    wait(act, q_done, i)
                    hi_of(G1, xT_hi, xt_done, xTh_ready)
                if attend:
                    exps(i - 1, 4)
                    exp_hi(i - 1, 3)
                if front:
                    act.wait_ge(ct_done, i + 1)
                    wait(act, v_done, i)
                    hi_of(G0, cT_hi, ct_done, cTh_ready)
                if attend:
                    exps(i - 1, 5)
                    exp_hi(i - 1, 4)
                    exps(i - 1, 6)
                    exp_hi(i - 1, 5)
                    exps(i - 1, 7)
                if front:
                    act.wait_ge(q_done, i + 1)
                    wait(act, ql_ready, i)
                    for a in range(KC):
                        last = nc.scalar.activation(q32[:, a, :], G1[:, a * 256:(a + 1) * 256], ACT.Identity,
                                                    bias=bq_col[:, a:a + 1])
                    last.then_inc(q32_ready, 1)
                    act.wait_ge(k_done, i + 1)
                    wait(act, kl_ready, i)
                    for a in range(KC):
                        last = nc.scalar.activation(k32[:, a, :], G0[:, a * 256:(a + 1) * 256], ACT.Identity,
                                                    bias=bk_col[:, a:a + 1])
                    last.then_inc(k32_ready, 1)
                if back2:
                    silu(i - 3, 0)
                    silu(i - 3, 1)
                if attend:
                    exp_hi(i - 1, 6)
                if back2:
                    silu(i - 3, 2)
                    silu(i - 3, 3)
                if attend:
                    exp_hi(i - 1, 7)
                if back2:
                    for e in range(4, EU):
                        silu(i - 3, e)

            run_steps(act, step)

        @block.vector
        def _(dve):
            v = nc.vector

            def lo_of(bank, hi, lo, hi_ready, value, ready):
                dve.wait_ge(hi_ready, value)
                v.tensor_tensor(lo[:, :, :, :], quad(bank), hi[:, :, :, :].bitcast(F32), ALU.subtract
                                ).then_inc(ready, 1)

            v.memset(w_nat[:, 5], 0.0).then_inc(w_cleared, 1)
            v.memset(gates[:, 0:1], 1.0)
            v.memset(half_neg[:], -0.5)
            v.memset(v_part[:, :, :, VC - 1:VC], 1.0)
            v.memset(gates[:, 3:4], SCALE).then_inc(gates_ready, 1)
            dve.wait_ge(ld_first, N_FIRST)
            v.tensor_copy(ident_bf[:], ident)
            for j in range(4):
                v.tensor_copy(causal_bf[:, j, :], cst[:, C_CAUSAL:C_CAUSAL + P])
            dve.wait_ge(gates_ready, 2)
            v.tensor_scalar(bq_col[:], bq_col[:], SCALE, None, ALU.mult)
            v.tensor_scalar(bo_row[:], bo_row[:], gates[:, 1:2], None, ALU.mult).then_inc(consts_ready, 2)
            dve.wait_ge(ld_rest, 16)
            v.tensor_copy(eb_part[:, 0, :], eb_nat[:]).then_inc(eb_step, 1)
            dve.wait_ge(eb_step, 1)
            v.tensor_tensor(eb_rest[:, 0, :], eb_nat[:], eb_part[:, 0, :], ALU.subtract).then_inc(eb_step, 1)
            dve.wait_ge(eb_step, 2)
            v.tensor_copy(eb_part[:, 1, :], eb_rest[:, 0, :]).then_inc(eb_step, 1)
            dve.wait_ge(eb_step, 3)
            v.tensor_tensor(eb_rest[:, 1, :], eb_rest[:, 0, :], eb_part[:, 1, :], ALU.subtract).then_inc(eb_step, 1)
            dve.wait_ge(eb_step, 4)
            v.tensor_copy(eb_part[:, 2, :], eb_rest[:, 1, :]).then_inc(eb_step, 1)
            for m in range(PREP):
                dve.wait_ge(w_hi_ready, m + 1)
                bank = banks[m % 8][:, :].rearrange("p (k c) -> p k c", k=KC)
                if m < 5:
                    src, hi, lo, g = bank, w_hi[:, m], w_lo[:, m], scale_of[m]
                elif m == 5:
                    src, hi, lo, g = bank[:, :, 0:P], gw_hi[:], gw_lo[:], 0
                else:
                    src, hi, lo, g = bank, ew_hi[:, :, m - 6, :], ew_lo[:, :, m - 6, :], 0
                v.scalar_tensor_tensor(out=lo, in0=src, scalar=gates[:, g:g + 1], in1=hi.bitcast(F32),
                                       op0=ALU.mult, op1=ALU.subtract).then_inc(w_lo_ready, 1)

            def ln_stats(src, st, mv, ve, step, n):
                for s in range(2):
                    last = v.bn_stats(st[:, s, :], src[:, s, :])
                last.then_inc(step, 1)
                wait_alone(dve, step, n + 1)
                for s in range(2):
                    last = v.bn_aggr(mv[:, s, :], st[:, s, :])
                last.then_inc(step, 1)
                dve.wait_ge(step, n + 2)
                v.tensor_scalar(ve[:], mv[:, :, 1], EPS, None, ALU.add).then_inc(step, 1)

            def ln_apply(dst, src, mv, rstd, ready):
                for s in range(2):
                    last = v.tensor_scalar(dst[:, s, :], src[:, s, :], mv[:, s, 0:1], rstd[:, s:s + 1],
                                           ALU.subtract, ALU.mult)
                last.then_inc(ready, 1)

            def row_max(p, u):
                dve.wait_ge(s_done, 8 * p + u + 1)
                v.tensor_reduce(neg_max[:, u, :], S[u % 2][:, :].rearrange("p (j t) -> p j t", j=4), AX_X,
                                ALU.max, negate=True).then_inc(max_ready, 1)

            def exp_lo(p, u):
                dve.wait_ge(eh_ready, 8 * p + u + 1)
                v.tensor_tensor(e_lo[:, u % 2, :, :], TB[:, :].rearrange("p (j t) -> p j t", j=4),
                                e_hi[:, u % 2, :, :], ALU.subtract).then_inc(el_ready, 1)

            def normalise(p, u):
                n = 4 * p + u // 2
                s, half = u // 4, u % 4 // 2
                dve.wait_ge(pv_done, 8 * p + u + 1)
                if u == 1:
                    wait(dve, ot_done, p)
                ob = OB[:, 0:8 * VC].rearrange("p (h c) -> p h c", c=VC)
                v.reciprocal(inv_sum[:].rearrange("p a h -> p (a h)"), ob[:, :, VC - 1])
                v.tensor_reduce(o_sum[:].rearrange("p a h d -> p (a h) d"), ob[:, :, 0:VC - 1].rearrange("p h (k d) -> p h d k", k=3), AX_X,
                                ALU.add).then_inc(norm_step, 1)
                dve.wait_ge(norm_step, n + 1)
                v.tensor_tensor(o_n[:, s, :, half, :, :], o_sum[:],
                                inv_sum[:].unsqueeze(3).broadcast_to([P, 2, 4, HD]), ALU.mult
                                ).then_inc(norm_ready, 1)

            def accumulate(p, e):
                s, f = divmod(e, 4)
                dve.wait_ge(silu_ready, 8 * p + e + 1)
                if e == 0:
                    wait(dve, mt_done, p)
                for j in range(2):
                    n = 16 * p + 2 * e + j
                    w = w_tok[:, s, 2 * f + j:2 * f + j + 1]
                    if f == 0 and j == 0:
                        ins = v.tensor_scalar(mix[:, s, :], act_e[:, e % 2, j, :], w, None, ALU.mult)
                    else:
                        dve.wait_ge(acc_step, n)
                        ins = v.scalar_tensor_tensor(out=mix[:, s, :], in0=act_e[:, e % 2, j, :], scalar=w,
                                                     in1=mix[:, s, :], op0=ALU.mult, op1=ALU.add)
                    ins.then_inc(acc_step, 1)

            def step(i):
                front, attend, back1, back2, back3 = stages(i)
                if back2:
                    lo_of(G0, x2T_hi, x2T_lo, x2h_ready, i - 2, x2l_ready)
                if attend:
                    row_max(i - 1, 0)
                if back3:
                    lo_of(G1, mT_hi, mT_lo, mTh_ready, i - 3, mTl_ready)
                if attend:
                    row_max(i - 1, 1)
                if front:
                    dve.wait_ge(x_loaded, 16 * (i + 1))
                    ln_stats(x_in, st1, mv1, ve1, ln1_step, 3 * i)
                if back1:
                    lo_of(G1, oT_hi, oT_lo, oTh_ready, i - 1, oTl_ready)
                if attend:
                    exp_lo(i - 1, 0)
                if back3:
                    dve.wait_ge(comb_done, i - 3)
                    dve.wait_ge(x1_copied, i - 3)
                    wait(dve, y_stored, 16 * (i - 4))
                    v.tensor_tensor(y[:, :, :], G0[:, :].rearrange("p (s c) -> p s c", s=2), x1_kept[:],
                                    ALU.add).then_inc(y_ready, 1)
                if attend:
                    row_max(i - 1, 2)
                if back2:
                    dve.wait_ge(gt_done, i - 2)
                    lg = G1[:, 0:256].rearrange("p (s t) -> p s t", s=2)[:, :, 0:NE]
                    v.tensor_reduce(r_max[:], lg, AX_X, ALU.max, negate=True).then_inc(rmax_ready, 1)
                    dve.wait_ge(rmax_ready, i - 2)
                    v.tensor_tensor(r_sub[:], lg, r_max[:].unsqueeze(2).broadcast_to([P, 2, NE]), ALU.add
                                    ).then_inc(rsub_ready, 1)
                if front:
                    dve.wait_ge(rstd1_ready, i + 1)
                    wait(dve, xt_done, i)
                    ln_apply(xn, x_in, mv1, rstd1, xn_ready)
                if attend:
                    exp_lo(i - 1, 1)
                if back1:
                    dve.wait_ge(p_done, i - 1)
                    dve.wait_ge(xb_ready, i - 1)
                    wait(dve, x1_copied, i - 2)
                    v.tensor_tensor(x1[:, :, :], G0[:, :].rearrange("p (s c) -> p s c", s=2), xb[:],
                                    ALU.add).then_inc(x1_ready, 1)
                if attend:
                    row_max(i - 1, 3)
                if back1:
                    dve.wait_ge(x1_ready, i - 1)
                    ln_stats(x1, st2, mv2, ve2, ln2_step, 3 * (i - 2))
                if attend:
                    normalise(i - 1, 1)
                    exp_lo(i - 1, 2)
                if back2:
                    n = 3 * (i - 3)
                    dve.wait_ge(rexp_ready, i - 2)
                    v.tensor_reduce(r_sum[:], r_exp[:], AX_X, ALU.add).then_inc(prob_step, 1)
                    dve.wait_ge(prob_step, n + 1)
                    v.reciprocal(r_inv[:], r_sum[:]).then_inc(prob_step, 1)
                    dve.wait_ge(prob_step, n + 2)
                    v.tensor_tensor(prob[:], r_exp[:], r_inv[:].unsqueeze(2).broadcast_to([P, 2, NE]),
                                    ALU.mult).then_inc(prob_step, 1)
                    dve.wait_ge(prob_step, n + 3)
                    of_j = prob[:].unsqueeze(2).broadcast_to([P, 2, NE, NE])
                    of_e = prob[:].unsqueeze(3).broadcast_to([P, 2, NE, NE])
                    v.tensor_tensor(cmp_gt[:], of_j, of_e, ALU.is_gt)
                    v.tensor_tensor(cmp_eq[:], of_j, of_e, ALU.is_equal).then_inc(cmp_ready, 1)
                if front:
                    lo_of(G1, xT_hi, xT_lo, xTh_ready, i + 1, xTl_ready)
                if attend:
                    row_max(i - 1, 4)
                if back1:
                    dve.wait_ge(rstd2_ready, i - 1)
                    wait(dve, x2t_done, i - 2)
                    ln_apply(xn2, x1, mv2, rstd2, xn2_ready)
                if attend:
                    exp_lo(i - 1, 3)
                if front:
                    lo_of(G0, cT_hi, cT_lo, cTh_ready, i + 1, cTl_ready)
                if attend:
                    row_max(i - 1, 5)
                    normalise(i - 1, 3)
                    exp_lo(i - 1, 4)
                    row_max(i - 1, 6)
                    exp_lo(i - 1, 5)
                    row_max(i - 1, 7)
                if back2:
                    n = 2 * (i - 3)
                    dve.wait_ge(cmp_step, 2 * (i - 2))
                    v.tensor_reduce(rank[:], cmp_gt[:], AX_X, ALU.add).then_inc(rank_step, 1)
                    dve.wait_ge(rank_step, n + 1)
                    v.scalar_tensor_tensor(out=w_tok[:], in0=rank[:], scalar=1.5, in1=prob[:],
                                           op0=ALU.is_lt, op1=ALU.mult).then_inc(rank_step, 1)
                if front:
                    dve.wait_ge(qh_ready, i + 1)
                    v.tensor_tensor(q_lo[:, :, :, :], q32[:, :, :].rearrange("p a (s t) -> p a s t", s=2),
                                    q_hi[:, :, :, :].bitcast(F32), ALU.subtract).then_inc(ql_ready, 1)
                    for r in range(2):
                        dve.wait_ge(kh_ready, 2 * i + r + 1)
                        for a in range(KC):
                            last = v.scalar_tensor_tensor(
                                out=k_lo[:, a, :, r, :], in0=k32[:, a, :].rearrange("p (s t) -> p s t", s=2),
                                scalar=parity[r], in1=k_hi[:, a, :, r, :].bitcast(F32),
                                op0=ALU.mult, op1=ALU.subtract)
                    last.then_inc(kl_ready, 1)
                if back2:
                    dve.wait_ge(rank_step, 2 * (i - 2))
                    accumulate(i - 3, 0)
                    accumulate(i - 3, 1)
                if attend:
                    normalise(i - 1, 5)
                    exp_lo(i - 1, 6)
                if back2:
                    accumulate(i - 3, 2)
                if front:
                    dve.wait_ge(v_done, i + 1)
                    wait(dve, v_split, 5 * i)
                    v.tensor_tensor(v32[:], G1[:, :].rearrange("p (s c) -> p s c", s=2),
                                    bv_row[:].unsqueeze(1).broadcast_to([P, 2, C]), ALU.add
                                    ).then_inc(v32_ready, 1)
                if back2:
                    accumulate(i - 3, 3)
                if attend:
                    exp_lo(i - 1, 7)
                if back2:
                    accumulate(i - 3, 4)
                if attend:
                    normalise(i - 1, 7)
                if back2:
                    for e in range(5, EU):
                        accumulate(i - 3, e)

            run_steps(dve, step)

        @block.gpsimd
        def _(pool):
            g = nc.gpsimd
            g.memset(bias_sel[:], 0.0).then_inc(pool_setup, 1)
            g.memset(ebias[:], 0.0).then_inc(pool_setup, 1)
            pool.wait_ge(pool_setup, 2)
            g.memset(bias_sel[0:3, :], 1.0).then_inc(pool_setup, 1)
            pool.wait_ge(consts_ready, 2)

            def heads(t):
                return t.rearrange("p s (h d) -> p s h d", d=HD)

            def round_to(dst, src):
                return g.tensor_scalar(dst, src, 1.0, 1.0, ALU.mult, ALU.mult)

            def step(i):
                front, attend, back1, back2, back3 = stages(i)
                if front:
                    pool.wait_ge(ln1_step, 3 * i + 3)
                    g.tensor_tensor(rstd1[:], ve1[:], half_neg[:], ALU.pow).then_inc(rstd1_ready, 1)
                if back1:
                    pool.wait_ge(res_loaded, 16 * (i - 1))
                    wait(pool, x1_ready, i - 2)
                    g.tensor_tensor(xb[:], x_res[:], bo_row[:].unsqueeze(1).broadcast_to([P, 2, C]), ALU.add
                                    ).then_inc(xb_ready, 1)
                if back2:
                    pool.wait_ge(x1_ready, i - 2)
                    wait_alone(pool, y_ready, i - 3)
                    g.tensor_scalar(x1_kept[:], x1[:], 1.0, 1.0, ALU.mult, ALU.mult).then_inc(x1_copied, 1)
                if back1:
                    pool.wait_ge(ln2_step, 3 * (i - 1))
                    g.tensor_tensor(rstd2[:], ve2[:], half_neg[:], ALU.pow).then_inc(rstd2_ready, 1)
                if back2:
                    pool.wait_ge(cmp_ready, i - 2)
                    low = cst[:, C_LOWER:C_LOWER + 64].rearrange("p (e j) -> p e j", e=NE).unsqueeze(1)
                    g.tensor_tensor(cmp_eq[:], cmp_eq[:], low.broadcast_to([P, 2, NE, NE]), ALU.mult
                                    ).then_inc(cmp_step, 1)
                    pool.wait_ge(cmp_step, 2 * (i - 3) + 1)
                    g.tensor_tensor(cmp_gt[:], cmp_gt[:], cmp_eq[:], ALU.add).then_inc(cmp_step, 1)
                if front:
                    pool.wait_ge(q32_ready, i + 1)
                    wait_alone(pool, s_done, 8 * i)
                    round_to(q_hi[:, :, :, :], q32[:, :, :].rearrange("p a (s t) -> p a s t", s=2)
                             ).then_inc(qh_ready, 1)
                    wait_alone(pool, k32_ready, i + 1)
                    for r in range(2):
                        for a in range(KC):
                            last = g.tensor_scalar(k_hi[:, a, :, r, :],
                                                   k32[:, a, :].rearrange("p (s t) -> p s t", s=2),
                                                   parity[r], 1.0, ALU.mult, ALU.mult)
                        last.then_inc(kh_ready, 1)
                    n = 5 * i
                    pool.wait_ge(v32_ready, i + 1)
                    wait_alone(pool, pv_done, 8 * i)
                    round_to(v_part[:, :, :, 0:HD], heads(v32[:])).then_inc(v_split, 1)
                    pool.wait_ge(v_split, n + 1)
                    g.tensor_tensor(heads(v_rest[:]), heads(v32[:]), v_part[:, :, :, 0:HD], ALU.subtract
                                    ).then_inc(v_split, 1)
                    wait_alone(pool, v_split, n + 2)
                    round_to(v_part[:, :, :, HD:2 * HD], heads(v_rest[:])).then_inc(v_split, 1)
                    pool.wait_ge(v_split, n + 3)
                    g.tensor_tensor(heads(v_rest[:]), heads(v_rest[:]), v_part[:, :, :, HD:2 * HD], ALU.subtract
                                    ).then_inc(v_split, 1)
                    wait_alone(pool, v_split, n + 4)
                    round_to(v_part[:, :, :, 2 * HD:3 * HD], heads(v_rest[:])).then_inc(v_split, 1)

            run_steps(pool, step)


_INS = ['x', 'ctx_1024', 'g_xattn', 'g_ffn', 'L0_xattn_wq', 'L0_xattn_bq', 'L0_xattn_wk', 'L0_xattn_bk',
        'L0_xattn_wv', 'L0_xattn_bv', 'L0_xattn_wo', 'L0_xattn_bo', 'L0_ffn_gate_w', 'L0_ffn_expert_w',
        'L0_ffn_expert_b', 'L0_ffn_combine_w']
_OUTS = [((64, 128, 256), 'float32')]


def kernel(**inputs):
    import numpy as _np
    import concourse.bacc as _bacc
    from concourse import mybir as _mybir
    from concourse.bass_utils import run_bass_kernel_spmd as _run

    nc = _bacc.Bacc("TRN2", target_bir_lowering=False, num_devices=1)
    arrays, args = {}, []
    for name in _INS:
        a = _np.ascontiguousarray(inputs[name])
        arrays[f"in_{name}_dram"] = a
        args.append(nc.dram_tensor(f"in_{name}_dram", a.shape, _mybir.dt.from_np(a.dtype), kind="ExternalInput").ap())
    c = _np.zeros((P, C_COLS), _np.float32)
    c[:, C_IDENT:C_IDENT + P] = _np.eye(P)
    c[:, C_CAUSAL:C_CAUSAL + P] = _np.triu(_np.full((P, P), -3.0e38), 1)
    c[:, C_PARITY] = _np.arange(P) // 16 % 2 == 0
    c[:, C_PARITY + 1] = _np.arange(P) // 16 % 2 == 1
    c[:, C_LOWER:C_LOWER + 64] = _np.tril(_np.ones((8, 8)), -1).reshape(1, 64)
    arrays["consts_dram"] = c
    args.append(nc.dram_tensor("consts_dram", c.shape, _mybir.dt.float32, kind="ExternalInput").ap())
    for i, (shape, dtype) in enumerate(_OUTS):
        dt = _mybir.dt.from_np(_np.dtype(dtype))
        args.append(nc.dram_tensor(f"out_{i}_dram", shape, dt, kind="ExternalOutput").ap())
    flamingo_block(nc, *args)
    r = _run(nc, [arrays], core_ids=[0])
    got = tuple(r.results[0][f"out_{i}_dram"] for i in range(len(_OUTS)))
    return got[0]
```

```python
from contextlib import ExitStack

import concourse.bass as bass
from concourse import mybir

P = 128
ALU = mybir.AluOpType
ACT = mybir.ActivationFunctionType
AX_X = mybir.AxisListType.X
F32 = mybir.dt.float32
F32R = mybir.dt.float32r
BF16 = mybir.dt.bfloat16
FP16 = mybir.dt.float16

C_IDENT = 0
C_CAUSAL = 128
C_PARITY = 256
C_LOWER = 258
C_COLS = 258 + 64


def flamingo_block(
    nc: bass.Bass,
    x: bass.AP,
    ctx_1024: bass.AP,
    g_xattn: bass.AP,
    g_ffn: bass.AP,
    L0_xattn_wq: bass.AP,
    L0_xattn_bq: bass.AP,
    L0_xattn_wk: bass.AP,
    L0_xattn_bk: bass.AP,
    L0_xattn_wv: bass.AP,
    L0_xattn_bv: bass.AP,
    L0_xattn_wo: bass.AP,
    L0_xattn_bo: bass.AP,
    L0_ffn_gate_w: bass.AP,
    L0_ffn_expert_w: bass.AP,
    L0_ffn_expert_b: bass.AP,
    L0_ffn_combine_w: bass.AP,
    consts: bass.AP,
    out: bass.AP,
):
    NSEQ, T, C = x.shape
    NPAIR = NSEQ // 2
    KC = C // P
    HD = 16
    H = C // HD
    NE = L0_ffn_expert_w.shape[0]
    VC = 3 * HD + 1
    SU = 8
    EU = 8
    SCALE = float(HD) ** -0.5
    EPS = 1e-5
    assert T == P and C == 2 * P and H == 16 and NE == 8

    with ExitStack() as ctx:
        def sb(name, shape, dt=F32):
            return ctx.enter_context(nc.sbuf_tensor(name, shape, dt))

        def sem(name):
            return ctx.enter_context(nc.semaphore(name))

        cst = sb("cst", [P, C_COLS])
        ident = cst[:, C_IDENT:C_IDENT + P]
        parity = [cst[:, C_PARITY + j:C_PARITY + j + 1] for j in range(2)]
        ident_bf = sb("ident_bf", [P, P], BF16)
        causal_bf = sb("causal_bf", [P, 4, P], BF16)
        half_neg = sb("half_neg", [P, 2])
        bias_sel = sb("bias_sel", [P, P], BF16)
        ebias = sb("ebias", [P, NE * C], BF16)
        eb_nat = sb("eb_nat", [16, P])
        eb_rest = sb("eb_rest", [16, 2, P])
        eb_part = sb("eb_part", [16, 3, P], BF16)
        gates = sb("gates", [P, 4])
        g_raw = sb("g_raw", [P, 2])
        bq_col = sb("bq_col", [P, KC])
        bk_col = sb("bk_col", [P, KC])
        bv_row = sb("bv_row", [P, C])
        bo_row = sb("bo_row", [P, C])
        w_nat = sb("w_nat", [P, 6 + NE, KC, C])
        w_hi = sb("w_hi", [P, 5, KC, C], F32R)
        w_lo = sb("w_lo", [P, 5, KC, C], F32R)
        gw_hi = sb("gw_hi", [P, KC, P], F32R)
        gw_lo = sb("gw_lo", [P, KC, P], F32R)
        ew_hi = sb("ew_hi", [P, KC, NE, C], F32R)
        ew_lo = sb("ew_lo", [P, KC, NE, C], F32R)

        x_in = sb("x_in", [P, 2, C])
        c_in = sb("c_in", [P, 2, C])
        x_res = sb("x_res", [P, 2, C])
        xb = sb("xb", [P, 2, C])
        st1 = sb("st1", [P, 2, 6])
        mv1 = sb("mv1", [P, 2, 2])
        ve1 = sb("ve1", [P, 2, 2])
        rs1 = sb("rs1", [P, 2, 2])
        xn = sb("xn", [P, 2, C])
        xT_hi = sb("xT_hi", [P, KC, 2, P], F32R)
        xT_lo = sb("xT_lo", [P, KC, 2, P], F32R)
        cT_hi = sb("cT_hi", [P, KC, 2, P], F32R)
        cT_lo = sb("cT_lo", [P, KC, 2, P], F32R)
        q32 = sb("q32", [P, KC, 2 * P])
        k32 = sb("k32", [P, KC, 2 * P])
        k_round = sb("k_round", [P, KC, 2 * P], F32R)
        k_rest = sb("k_rest", [P, KC, 2 * P])
        q_hi = sb("q_hi", [P, KC, 2, P], F32R)
        q_lo = sb("q_lo", [P, KC, 2, P], F32R)
        k_hi = sb("k_hi", [P, KC, 2, 2, P], F32R)
        k_lo = sb("k_lo", [P, KC, 2, 2, P], F32R)
        v_raw = sb("v_raw", [P, 2, C])
        v32 = sb("v32", [P, 2, C])
        v_rest = sb("v_rest", [P, 2, C])
        v_part = sb("v_part", [P, 2, H, VC], BF16)
        neg_max = sb("neg_max", [P, SU, 4])
        e_q = sb("e_q", [P, 4, 4, P])
        e_hi = sb("e_hi", [P, 2, 4, P], FP16)
        e_lo = sb("e_lo", [P, 2, 4, P], FP16)
        inv_sum = sb("inv_sum", [P, 2, 4])
        o_sum = sb("o_sum", [P, 2, 4, HD])
        o_n = sb("o_n", [P, 2, 2, 2, 4, HD])
        oT_hi = sb("oT_hi", [P, KC, 2, P], F32R)
        oT_lo = sb("oT_lo", [P, KC, 2, P], F32R)
        x1 = sb("x1", [P, 2, C])
        x1_kept = sb("x1_kept", [P, 2, C])
        st2 = sb("st2", [P, 2, 6])
        mv2 = sb("mv2", [P, 2, 2])
        ve2 = sb("ve2", [P, 2, 2])
        rs2 = sb("rs2", [P, 2, 2])
        xn2 = sb("xn2", [P, 2, C])
        x2T_hi = sb("x2T_hi", [P, KC, 2, P], F32R)
        x2T_lo = sb("x2T_lo", [P, KC, 2, P], F32R)
        lgT = sb("lgT", [P, 2, P])
        r_max = sb("r_max", [P, 2])
        r_sub = sb("r_sub", [P, 2, NE])
        r_exp = sb("r_exp", [P, 2, NE])
        r_sum = sb("r_sum", [P, 2])
        r_inv = sb("r_inv", [P, 2])
        prob = sb("prob", [P, 2, NE])
        cmp_gt = sb("cmp_gt", [P, 2, NE, NE])
        cmp_eq = sb("cmp_eq", [P, 2, NE, NE])
        rank = sb("rank", [P, 2, NE])
        w_tok = sb("w_tok", [P, 2, NE])
        act_e = sb("act_e", [P, 4, 2, C])
        mix = sb("mix", [P, 2, C])
        mT_hi = sb("mT_hi", [P, KC, 2, P], F32R)
        mT_lo = sb("mT_lo", [P, KC, 2, P], F32R)
        y = sb("y", [P, 2, C])

        banks = [ctx.enter_context(nc.psum_tensor(f"bank{i}", [P, 512], F32)) for i in range(8)]
        S = [banks[0], banks[1]]
        TB = banks[2]
        OB = banks[3]
        E = [banks[4], banks[5]]
        G0, G1 = banks[6], banks[7]

        def quad(b):
            return b[:, :].rearrange("p (a s t) -> p a s t", a=2, s=2)

        ld_first = sem("ld_first")
        ld_rest = sem("ld_rest")
        ld_experts = sem("ld_experts")
        w_cleared = sem("w_cleared")
        gates_ready = sem("gates_ready")
        w_transposed = sem("w_transposed")
        w_hi_ready = sem("w_hi_ready")
        w_lo_ready = sem("w_lo_ready")
        ew_transposed = sem("ew_transposed")
        ew_hi_ready = sem("ew_hi_ready")
        ew_lo_ready = sem("ew_lo_ready")
        consts_ready = sem("consts_ready")
        pool_setup = sem("pool_setup")
        eb_step = sem("eb_step")
        ebias_ready = sem("ebias_ready")

        x_loaded = sem("x_loaded")
        c_loaded = sem("c_loaded")
        res_loaded = sem("res_loaded")
        y_stored = sem("y_stored")
        ln1_step = sem("ln1_step")
        rs1_step = sem("rs1_step")
        xn_ready = sem("xn_ready")
        xt_done = sem("xt_done")
        xTh_ready = sem("xTh_ready")
        xTl_ready = sem("xTl_ready")
        ct_done = sem("ct_done")
        cTh_ready = sem("cTh_ready")
        cTl_ready = sem("cTl_ready")
        q_done = sem("q_done")
        q32_ready = sem("q32_ready")
        q_split = sem("q_split")
        k_done = sem("k_done")
        k32_ready = sem("k32_ready")
        k_rounded = sem("k_rounded")
        k_split = sem("k_split")
        v_done = sem("v_done")
        v_raw_ready = sem("v_raw_ready")
        v_split = sem("v_split")
        s_done = sem("s_done")
        max_ready = sem("max_ready")
        exp_ready = sem("exp_ready")
        t_done = sem("t_done")
        eh_ready = sem("eh_ready")
        el_ready = sem("el_ready")
        pv_done = sem("pv_done")
        norm_step = sem("norm_step")
        norm_ready = sem("norm_ready")
        ot_done = sem("ot_done")
        oTh_ready = sem("oTh_ready")
        oTl_ready = sem("oTl_ready")
        p_done = sem("p_done")
        xb_ready = sem("xb_ready")
        x1_ready = sem("x1_ready")
        x1_copied = sem("x1_copied")
        ln2_step = sem("ln2_step")
        rs2_step = sem("rs2_step")
        xn2_ready = sem("xn2_ready")
        x2t_done = sem("x2t_done")
        x2h_ready = sem("x2h_ready")
        x2l_ready = sem("x2l_ready")
        gl_done = sem("gl_done")
        lgT_ready = sem("lgT_ready")
        gt_done = sem("gt_done")
        rmax_ready = sem("rmax_ready")
        rsub_ready = sem("rsub_ready")
        rexp_ready = sem("rexp_ready")
        prob_step = sem("prob_step")
        cmp_ready = sem("cmp_ready")
        cmp_step = sem("cmp_step")
        rank_step = sem("rank_step")
        e_done = sem("e_done")
        silu_ready = sem("silu_ready")
        acc_step = sem("acc_step")
        mt_done = sem("mt_done")
        mTh_ready = sem("mTh_ready")
        mTl_ready = sem("mTl_ready")
        comb_done = sem("comb_done")
        y_ready = sem("y_ready")

        def wait(eng, s, value):
            if not (isinstance(value, int) and value <= 0):
                eng.wait_ge(s, value)

        def wait_alone(eng, s, value):
            wait(eng, s, value)
            eng.nop(nofuse=True)

        def stages(i):
            if not isinstance(i, int):
                return True, True, True, True
            return tuple(0 <= i - d < NPAIR for d in range(4))

        FILL = 4

        def run_steps(eng, step):
            for i in range(FILL):
                step(i)
            with eng.Fori(FILL, NPAIR) as i:
                step(i)
            for i in range(NPAIR, NPAIR + 3):
                step(i)

        attn_w = [L0_xattn_wq, L0_xattn_wk, L0_xattn_wv, L0_xattn_wo, L0_ffn_combine_w]
        scale_of = [3, 0, 0, 1, 2]
        WQ, WK, WV, WO, WC = range(5)
        x_pairs = x.rearrange("(i s) p c -> i p s c", s=2)
        c_pairs = ctx_1024.rearrange("(i s) p c -> i p s c", s=2)
        out_pairs = out.rearrange("(i s) p c -> i p s c", s=2)
        N_FIRST = 16 * (2 + 2 + len(attn_w) + 4)

        block = ctx.enter_context(nc.Block())

        @block.sync
        def _(sp):
            sp.dma_start(cst[:], consts).then_inc(ld_first, 16)
            for j, w in enumerate(attn_w):
                sp.dma_start(w_nat[:, j], w.rearrange("(a p) c -> p a c", p=P)).then_inc(ld_first, 16)
            sp.wait_ge(w_cleared, 1)
            sp.dma_start(w_nat[0:NE, 5, 0, :], L0_ffn_gate_w).then_inc(ld_first, 16)
            for j, g in enumerate((g_xattn, g_ffn)):
                sp.dma_start(g_raw[:, j:j + 1], g.rearrange("(o n) -> o n", o=1).broadcast_to([P, 1])
                             ).then_inc(ld_first, 16)
            for col, b in ((bq_col, L0_xattn_bq), (bk_col, L0_xattn_bk)):
                sp.dma_start(col[:], b.rearrange("(a p) -> p a", p=P), allow_slow_non_contiguous=True).then_inc(ld_first, 16)
            for row, b in ((bv_row, L0_xattn_bv), (bo_row, L0_xattn_bo)):
                sp.dma_start(row[:], b.rearrange("(o n) -> o n", o=1).broadcast_to([P, C])
                             ).then_inc(ld_first, 16)
            sp.dma_start(eb_nat[:], L0_ffn_expert_b.rearrange("e (h c) -> (e h) c", c=P)).then_inc(ld_rest, 16)

            def step(i):
                front, _, back, combine = stages(i)
                if back:
                    wait(sp, xb_ready, i - 2)
                    sp.dma_start(x_res[:], x_pairs[i - 2]).then_inc(res_loaded, 16)
                if front:
                    wait(sp, xn_ready, i)
                    sp.dma_start(x_in[:], x_pairs[i]).then_inc(x_loaded, 16)
                    wait(sp, ct_done, i)
                    sp.dma_start(c_in[:], c_pairs[i]).then_inc(c_loaded, 16)
                if isinstance(i, int) and i == 0:
                    for e in range(NE):
                        sp.dma_start(w_nat[:, 6 + e], L0_ffn_expert_w[e].rearrange("(a p) c -> p a c", p=P)
                                     ).then_inc(ld_experts, 16)
                    sp.wait_ge(eb_step, 5)
                    sp.wait_ge(pool_setup, 2)
                    for k in range(3):
                        sp.dma_start(ebias[k:k + 1, :].rearrange("o (h c) -> o h c", c=P),
                                     eb_part[:, k, :]).then_inc(ebias_ready, 16)
                if combine:
                    wait(sp, y_ready, i - 2)
                    sp.dma_start(out_pairs[i - 3], y[:]).then_inc(y_stored, 16)

            run_steps(sp, step)
            sp.wait_ge(y_stored, 16 * NPAIR)

        @block.tensor
        def _(pe):
            mm = nc.tensor.matmul

            def transpose4(bank, src, done):
                for s in range(2):
                    for a in range(KC):
                        last = nc.tensor.transpose(quad(bank)[:, a, s, :], src[:, s, a * P:(a + 1) * P], ident)
                last.then_inc(done, 1)

            def project_T(bank, w, hi, lo, done):
                for a in range(KC):
                    terms = [(l[:, w, kc, a * P:(a + 1) * P], r[:, kc, :, :])
                             for l, r in ((w_hi, hi), (w_hi, lo), (w_lo, hi)) for kc in range(KC)]
                    for n, (l, r) in enumerate(terms):
                        last = mm(bank[:, a * 256:(a + 1) * 256], l, r, start=n == 0, stop=n == len(terms) - 1)
                last.then_inc(done, 1)

            def project(bank, w, hi, lo, done):
                for s in range(2):
                    terms = [(l[:, kc, s, :], r[:, w, kc, :])
                             for l, r in ((hi, w_hi), (hi, w_lo), (lo, w_hi)) for kc in range(KC)]
                    for n, (l, r) in enumerate(terms):
                        last = mm(bank[:, s * 256:(s + 1) * 256], l, r, start=n == 0, stop=n == len(terms) - 1)
                last.then_inc(done, 1)

            def scores(p, u):
                s, g = divmod(u, 4)
                rows = slice(32 * g, 32 * g + 32)
                bank = S[u % 2]
                if u == 0:
                    pe.wait_ge(q_split, 2 * p + 2)
                    pe.wait_ge(k_split, p + 1)
                wait(pe, exp_ready, 8 * p + u - 1)
                mm(bank[:, :], ident_bf[:], causal_bf[:], start=True, stop=False, skip_group_check=True)
                for a in range(KC):
                    for n, (l, r) in enumerate(((q_hi, k_hi), (q_lo, k_hi), (q_hi, k_lo))):
                        last = mm(bank[:, a * 256:(a + 1) * 256], l[rows, a, s, :],
                                  r[rows, a, s, :, :], start=False, stop=n == 2, skip_group_check=True)
                last.then_inc(s_done, 1)

            def transposed_exp(p, u):
                pe.wait_ge(exp_ready, 8 * p + u + 1)
                wait(pe, el_ready, 8 * p + u)
                for j in range(4):
                    last = nc.tensor.transpose(TB[:, j * P:(j + 1) * P], e_q[:, u % 4, j, :], ident)
                last.then_inc(t_done, 1)

            def times_v(p, u):
                s, g = divmod(u, 4)
                if u == 0:
                    pe.wait_ge(v_split, 6 * p + 6)
                pe.wait_ge(el_ready, 8 * p + u + 1)
                if u % 2 == 0:
                    wait(pe, norm_ready, 4 * p + u // 2)
                for j in range(4):
                    a, odd = divmod(j, 2)
                    c0 = (4 * a + 2 * (u % 2) + odd) * VC
                    v = v_part[:, s, 8 * a + 2 * g + odd, :]
                    mm(OB[:, c0:c0 + VC], e_hi[:, u % 2, j, :], v, start=True, stop=False)
                    last = mm(OB[:, c0:c0 + VC], e_lo[:, u % 2, j, :], v, start=False, stop=True)
                last.then_inc(pv_done, 1)

            def expert_pair(p, e):
                f, s = divmod(e, 2)
                bank = E[e % 2]
                if e == 0:
                    pe.wait_ge(x2l_ready, p + 1)
                wait(pe, silu_ready, 8 * p + e - 1)
                mm(bank[:, :], bias_sel[:], ebias[:, f * 512:(f + 1) * 512], start=True, stop=False)
                terms = [(l[:, kc, s, :], r[:, kc, 2 * f:2 * f + 2, :])
                         for kc in range(KC) for l, r in ((x2T_hi, ew_hi), (x2T_hi, ew_lo), (x2T_lo, ew_hi))]
                for n, (l, r) in enumerate(terms):
                    last = mm(bank[:, :], l, r, start=False, stop=n == len(terms) - 1)
                last.then_inc(e_done, 1)

            def prepare(bank, m, done):
                for a in range(1 if m == 5 else KC):
                    for kc in range(KC):
                        o = bank[:, kc * C + a * P:kc * C + (a + 1) * P]
                        last = nc.tensor.transpose(o, w_nat[:, m, a, kc * P:(kc + 1) * P], ident)
                last.then_inc(done, 1)

            pe.wait_ge(ld_first, N_FIRST)
            for m in range(6):
                prepare(banks[m], m, w_transposed)
            pe.wait_ge(w_lo_ready, 6)
            pe.wait_ge(consts_ready, 2)

            def prepare_experts():
                pe.wait_ge(ld_experts, 16 * NE)
                for e in range(NE):
                    if e >= 2:
                        pe.wait_ge(ew_lo_ready, e - 1)
                    prepare(E[e % 2], 6 + e, ew_transposed)
                pe.wait_ge(ew_lo_ready, NE)
                pe.wait_ge(pool_setup, 3)
                pe.wait_ge(ebias_ready, 48)

            def step(i):
                front, attend, back, combine = stages(i)
                f, a, b, c = i, i - 1, i - 2, i - 3
                fixed = isinstance(i, int)
                if not fixed or 0 <= i - 3 < NPAIR:
                    pe.wait_ge(rsub_ready, i - 2)
                elif i >= 1:
                    pe.wait_ge(xTl_ready, i)
                if not fixed or 1 <= i <= NPAIR:
                    pe.wait_ge(v_raw_ready, i)
                elif i > NPAIR:
                    pe.wait_ge(y_ready, i - 3)

                if back:
                    pe.wait_ge(norm_ready, 4 * b + 4)
                    transpose4(G0, o_n[:].rearrange("p s a b h d -> p s (a b h d)"), ot_done)
                if attend:
                    scores(a, 0)
                    scores(a, 1)
                if combine:
                    pe.wait_ge(acc_step, 16 * c + 16)
                    transpose4(G1, mix, mt_done)
                if back:
                    pe.wait_ge(oTl_ready, b + 1)
                    project(G0, WO, oT_hi, oT_lo, p_done)
                if attend:
                    transposed_exp(a, 0)
                    scores(a, 2)
                    transposed_exp(a, 1)
                    times_v(a, 0)
                if combine:
                    pe.wait_ge(mTl_ready, c + 1)
                    project(G1, WC, mT_hi, mT_lo, comb_done)
                if attend:
                    scores(a, 3)
                    transposed_exp(a, 2)
                    times_v(a, 1)
                if front:
                    pe.wait_ge(xn_ready, f + 1)
                    if back:
                        pe.wait_ge(x1_ready, b + 1)
                    transpose4(G0, xn, xt_done)
                if attend:
                    scores(a, 4)
                if front:
                    pe.wait_ge(c_loaded, 16 * f + 16)
                    if combine:
                        pe.wait_ge(y_ready, c + 1)
                    transpose4(G1, c_in, ct_done)
                if attend:
                    transposed_exp(a, 3)
                    times_v(a, 2)
                if back:
                    pe.wait_ge(xn2_ready, b + 1)
                    if front:
                        pe.wait_ge(xTl_ready, f + 1)
                    transpose4(G0, xn2, x2t_done)
                if attend:
                    scores(a, 5)
                if front:
                    pe.wait_ge(xTl_ready, f + 1)
                    pe.wait_ge(cTl_ready, f + 1)
                    project_T(G1, WQ, xT_hi, xT_lo, q_done)
                if attend:
                    transposed_exp(a, 4)
                    times_v(a, 3)
                    scores(a, 6)
                if back:
                    pe.wait_ge(x2l_ready, b + 1)
                    for n, (l, r) in enumerate(((gw_hi, x2T_hi), (gw_hi, x2T_lo), (gw_lo, x2T_hi))):
                        for kc in range(KC):
                            last = mm(G0[:, 0:256], l[:, kc, :], r[:, kc, :, :],
                                      start=n == 0 and kc == 0, stop=n == 2 and kc == 1)
                    last.then_inc(gl_done, 1)
                if attend:
                    transposed_exp(a, 5)
                    times_v(a, 4)
                if front:
                    pe.wait_ge(q32_ready, f + 1)
                    project_T(G1, WK, cT_hi, cT_lo, k_done)
                if attend:
                    scores(a, 7)
                if back:
                    pe.wait_ge(lgT_ready, b + 1)
                    for s in range(2):
                        last = nc.tensor.transpose(G0[:, s * P:(s + 1) * P], lgT[:, s, :], ident)
                    last.then_inc(gt_done, 1)
                if attend:
                    transposed_exp(a, 6)
                    times_v(a, 5)
                if back:
                    expert_pair(b, 0)
                if attend:
                    transposed_exp(a, 7)
                    times_v(a, 6)
                if front:
                    pe.wait_ge(k32_ready, f + 1)
                    project(G1, WV, cT_hi, cT_lo, v_done)
                if back:
                    expert_pair(b, 1)
                if attend:
                    times_v(a, 7)
                if fixed and i == 0:
                    prepare_experts()
                if back:
                    for e in range(2, EU):
                        expert_pair(b, e)

            run_steps(pe, step)

        @block.scalar
        def _(act):
            def hi_of(bank, dst, ready):
                nc.scalar.activation(dst[:, :, :, :], quad(bank), ACT.Copy).then_inc(ready, 1)

            act.wait_ge(ld_first, N_FIRST)
            nc.scalar.activation(gates[:, 1:3], g_raw[:], ACT.Tanh).then_inc(gates_ready, 1)
            act.wait_ge(gates_ready, 2)
            for m in range(6):
                act.wait_ge(w_transposed, m + 1)
                src = banks[m][:, :].rearrange("p (k c) -> p k c", k=KC)
                dst, g = (w_hi[:, m], scale_of[m]) if m < 5 else (gw_hi[:], 0)
                if m == 5:
                    src = src[:, :, 0:P]
                nc.scalar.activation(dst, src, ACT.Copy, scale=gates[:, g:g + 1]).then_inc(w_hi_ready, 1)

            def prepare_experts():
                for e in range(NE):
                    act.wait_ge(ew_transposed, e + 1)
                    nc.scalar.activation(ew_hi[:, :, e, :], E[e % 2][:, :].rearrange("p (k c) -> p k c", k=KC),
                                         ACT.Copy).then_inc(ew_hi_ready, 1)

            def normed(dst, src, rs, ready):
                for s in range(2):
                    last = nc.scalar.activation(dst[:, s, :], src[:, s, :], ACT.Identity,
                                                scale=rs[:, 0, s:s + 1], bias=rs[:, 1, s:s + 1])
                last.then_inc(ready, 1)

            def exps(p, u):
                act.wait_ge(max_ready, 8 * p + u + 1)
                wait(act, t_done, 8 * p + u - 3)
                for j in range(4):
                    last = nc.scalar.activation(e_q[:, u % 4, j, :], S[u % 2][:, j * P:(j + 1) * P], ACT.Exp,
                                                bias=neg_max[:, u, j:j + 1])
                last.then_inc(exp_ready, 1)

            def exp_hi(p, u):
                act.wait_ge(t_done, 8 * p + u + 1)
                wait(act, pv_done, 8 * p + u - 1)
                nc.scalar.activation(e_hi[:, u % 2, :, :], TB[:, :].rearrange("p (j t) -> p j t", j=4),
                                     ACT.Copy).then_inc(eh_ready, 1)

            def silu(p, e):
                act.wait_ge(e_done, 8 * p + e + 1)
                wait(act, acc_step, 16 * p + 4 * (e // 2 - 1))
                nc.scalar.activation(act_e[:, e % 4, :, :], E[e % 2][:, :].rearrange("p (f c) -> p f c", f=2),
                                     ACT.Silu).then_inc(silu_ready, 1)

            def step(i):
                front, attend, back, combine = stages(i)
                f, a, b, c = i, i - 1, i - 2, i - 3
                if back:
                    act.wait_ge(ot_done, b + 1)
                    wait(act, p_done, b)
                    hi_of(G0, oT_hi, oTh_ready)
                if attend:
                    exps(a, 0)
                if combine:
                    act.wait_ge(mt_done, c + 1)
                    wait(act, comb_done, c)
                    hi_of(G1, mT_hi, mTh_ready)
                if attend:
                    exps(a, 1)
                if front:
                    act.wait_ge(rs1_step, 2 * f + 2)
                    wait(act, xt_done, f)
                    normed(xn, x_in, rs1, xn_ready)
                if attend:
                    exp_hi(a, 0)
                    exps(a, 2)
                    exp_hi(a, 1)
                    exps(a, 3)
                    exp_hi(a, 2)
                if back:
                    act.wait_ge(rs2_step, 2 * b + 2)
                    wait(act, x2t_done, b)
                    normed(xn2, x1, rs2, xn2_ready)
                if front:
                    act.wait_ge(xt_done, f + 1)
                    wait(act, q_done, f)
                    hi_of(G0, xT_hi, xTh_ready)
                if attend:
                    exps(a, 4)
                if front:
                    act.wait_ge(ct_done, f + 1)
                    wait(act, v_done, f)
                    hi_of(G1, cT_hi, cTh_ready)
                if attend:
                    exp_hi(a, 3)
                if back:
                    act.wait_ge(x2t_done, b + 1)
                    wait(act, e_done, 8 * b)
                    hi_of(G0, x2T_hi, x2h_ready)
                if attend:
                    exps(a, 5)
                if front:
                    act.wait_ge(q_done, f + 1)
                    wait(act, q_split, 2 * f)
                    for k in range(KC):
                        last = nc.scalar.activation(q32[:, k, :], G1[:, k * 256:(k + 1) * 256], ACT.Identity,
                                                    bias=bq_col[:, k:k + 1])
                    last.then_inc(q32_ready, 1)
                if attend:
                    exp_hi(a, 4)
                    exps(a, 6)
                if back:
                    act.wait_ge(gl_done, b + 1)
                    wait(act, gt_done, b)
                    nc.scalar.activation(lgT[:], G0[:, 0:256].rearrange("p (s t) -> p s t", s=2),
                                         ACT.Copy).then_inc(lgT_ready, 1)
                if attend:
                    exp_hi(a, 5)
                if front:
                    act.wait_ge(k_done, f + 1)
                    wait(act, k_rounded, 2 * f)
                    for k in range(KC):
                        last = nc.scalar.activation(k32[:, k, :], G1[:, k * 256:(k + 1) * 256], ACT.Identity,
                                                    bias=bk_col[:, k:k + 1])
                    last.then_inc(k32_ready, 1)
                if attend:
                    exps(a, 7)
                    exp_hi(a, 6)
                if back:
                    act.wait_ge(rsub_ready, b + 1)
                    nc.scalar.activation(r_exp[:], r_sub[:], ACT.Exp).then_inc(rexp_ready, 1)
                    silu(b, 0)
                if attend:
                    exp_hi(a, 7)
                if front:
                    act.wait_ge(v_done, f + 1)
                    wait(act, v_split, 6 * f - 5)
                    nc.scalar.activation(v_raw[:], G1[:, :].rearrange("p (s c) -> p s c", s=2), ACT.Copy
                                         ).then_inc(v_raw_ready, 1)
                if isinstance(i, int) and i == 0:
                    prepare_experts()
                if back:
                    for e in range(1, EU):
                        silu(b, e)

            run_steps(act, step)

        @block.vector
        def _(dve):
            v = nc.vector

            def lo_of(bank, hi, lo, hi_ready, value, ready):
                dve.wait_ge(hi_ready, value)
                v.tensor_tensor(lo[:, :, :, :], quad(bank), hi[:, :, :, :].bitcast(F32), ALU.subtract
                                ).then_inc(ready, 1)

            v.memset(w_nat[:, 5], 0.0).then_inc(w_cleared, 1)
            v.memset(gates[:, 0:1], 1.0)
            v.memset(half_neg[:], -0.5)
            v.memset(v_part[:, :, :, VC - 1:VC], 1.0)
            v.memset(gates[:, 3:4], SCALE).then_inc(gates_ready, 1)
            dve.wait_ge(ld_first, N_FIRST)
            v.tensor_copy(ident_bf[:], ident)
            for j in range(4):
                v.tensor_copy(causal_bf[:, j, :], cst[:, C_CAUSAL:C_CAUSAL + P])
            dve.wait_ge(gates_ready, 2)
            v.tensor_scalar(bq_col[:], bq_col[:], SCALE, None, ALU.mult)
            v.tensor_scalar(bo_row[:], bo_row[:], gates[:, 1:2], None, ALU.mult).then_inc(consts_ready, 2)
            dve.wait_ge(ld_rest, 16)
            v.tensor_copy(eb_part[:, 0, :], eb_nat[:]).then_inc(eb_step, 1)
            dve.wait_ge(eb_step, 1)
            v.tensor_tensor(eb_rest[:, 0, :], eb_nat[:], eb_part[:, 0, :], ALU.subtract).then_inc(eb_step, 1)
            dve.wait_ge(eb_step, 2)
            v.tensor_copy(eb_part[:, 1, :], eb_rest[:, 0, :]).then_inc(eb_step, 1)
            dve.wait_ge(eb_step, 3)
            v.tensor_tensor(eb_rest[:, 1, :], eb_rest[:, 0, :], eb_part[:, 1, :], ALU.subtract).then_inc(eb_step, 1)
            dve.wait_ge(eb_step, 4)
            v.tensor_copy(eb_part[:, 2, :], eb_rest[:, 1, :]).then_inc(eb_step, 1)
            for m in range(6):
                dve.wait_ge(w_hi_ready, m + 1)
                src = banks[m][:, :].rearrange("p (k c) -> p k c", k=KC)
                hi, lo, g = (w_hi[:, m], w_lo[:, m], scale_of[m]) if m < 5 else (gw_hi[:], gw_lo[:], 0)
                if m == 5:
                    src = src[:, :, 0:P]
                v.scalar_tensor_tensor(out=lo, in0=src, scalar=gates[:, g:g + 1], in1=hi.bitcast(F32),
                                       op0=ALU.mult, op1=ALU.subtract).then_inc(w_lo_ready, 1)

            def prepare_experts():
                for e in range(NE):
                    dve.wait_ge(ew_hi_ready, e + 1)
                    v.tensor_tensor(ew_lo[:, :, e, :], E[e % 2][:, :].rearrange("p (k c) -> p k c", k=KC),
                                    ew_hi[:, :, e, :].bitcast(F32), ALU.subtract).then_inc(ew_lo_ready, 1)

            def ln_stats(src, st, mv, ve, step, n):
                for s in range(2):
                    last = v.bn_stats(st[:, s, :], src[:, s, :])
                last.then_inc(step, 1)
                wait_alone(dve, step, n + 1)
                for s in range(2):
                    last = v.bn_aggr(mv[:, s, :], st[:, s, :])
                last.then_inc(step, 1)
                dve.wait_ge(step, n + 2)
                v.tensor_scalar(ve[:, 0, :], mv[:, :, 1], EPS, None, ALU.add)
                v.tensor_scalar(ve[:, 1, :], mv[:, :, 0], -1.0, None, ALU.mult).then_inc(step, 1)

            def row_max(p, u):
                dve.wait_ge(s_done, 8 * p + u + 1)
                v.tensor_reduce(neg_max[:, u, :], S[u % 2][:, :].rearrange("p (j t) -> p j t", j=4), AX_X,
                                ALU.max, negate=True).then_inc(max_ready, 1)

            def exp_lo(p, u):
                dve.wait_ge(eh_ready, 8 * p + u + 1)
                v.tensor_tensor(e_lo[:, u % 2, :, :], TB[:, :].rearrange("p (j t) -> p j t", j=4),
                                e_hi[:, u % 2, :, :], ALU.subtract).then_inc(el_ready, 1)

            def normalise(p, u):
                n = 4 * p + u // 2
                s, half = u // 4, u % 4 // 2
                dve.wait_ge(pv_done, 8 * p + u + 1)
                if u == 1:
                    wait(dve, ot_done, p)
                ob = OB[:, 0:8 * VC].rearrange("p (h c) -> p h c", c=VC)
                v.reciprocal(inv_sum[:].rearrange("p a h -> p (a h)"), ob[:, :, VC - 1])
                v.tensor_reduce(o_sum[:].rearrange("p a h d -> p (a h) d"), ob[:, :, 0:VC - 1].rearrange("p h (k d) -> p h d k", k=3), AX_X,
                                ALU.add).then_inc(norm_step, 1)
                dve.wait_ge(norm_step, n + 1)
                v.tensor_tensor(o_n[:, s, :, half, :, :], o_sum[:],
                                inv_sum[:].unsqueeze(3).broadcast_to([P, 2, 4, HD]), ALU.mult
                                ).then_inc(norm_ready, 1)

            def accumulate(p, f):
                dve.wait_ge(silu_ready, 8 * p + 2 * f + 2)
                if f == 0:
                    wait(dve, mt_done, p)
                for j in range(2):
                    for s in range(2):
                        n = 16 * p + 4 * f + 2 * j + s
                        w = w_tok[:, s, 2 * f + j:2 * f + j + 1]
                        term = act_e[:, (2 * f + s) % 4, j, :]
                        if f == 0 and j == 0:
                            ins = v.tensor_scalar(mix[:, s, :], term, w, None, ALU.mult)
                        else:
                            dve.wait_ge(acc_step, n - 1)
                            ins = v.scalar_tensor_tensor(out=mix[:, s, :], in0=term, scalar=w,
                                                         in1=mix[:, s, :], op0=ALU.mult, op1=ALU.add)
                        ins.then_inc(acc_step, 1)

            def step(i):
                front, attend, back, combine = stages(i)
                f, a, b, c = i, i - 1, i - 2, i - 3
                if front:
                    dve.wait_ge(x_loaded, 16 * f + 16)
                    ln_stats(x_in, st1, mv1, ve1, ln1_step, 3 * f)
                if back:
                    lo_of(G0, oT_hi, oT_lo, oTh_ready, b + 1, oTl_ready)
                if attend:
                    row_max(a, 0)
                    row_max(a, 1)
                if combine:
                    lo_of(G1, mT_hi, mT_lo, mTh_ready, c + 1, mTl_ready)
                if back:
                    dve.wait_ge(p_done, b + 1)
                    dve.wait_ge(xb_ready, b + 1)
                    wait(dve, x1_copied, b)
                    v.tensor_tensor(x1[:, :, :], G0[:, :].rearrange("p (s c) -> p s c", s=2), xb[:],
                                    ALU.add).then_inc(x1_ready, 1)
                if attend:
                    exp_lo(a, 0)
                if back:
                    dve.wait_ge(x1_ready, b + 1)
                    ln_stats(x1, st2, mv2, ve2, ln2_step, 3 * b)
                if attend:
                    row_max(a, 2)
                    exp_lo(a, 1)
                if combine:
                    dve.wait_ge(comb_done, c + 1)
                    dve.wait_ge(x1_copied, c + 1)
                    wait(dve, y_stored, 16 * c)
                    v.tensor_tensor(y[:, :, :], G1[:, :].rearrange("p (s c) -> p s c", s=2), x1_kept[:],
                                    ALU.add).then_inc(y_ready, 1)
                if attend:
                    row_max(a, 3)
                    exp_lo(a, 2)
                    normalise(a, 1)
                if front:
                    lo_of(G0, xT_hi, xT_lo, xTh_ready, f + 1, xTl_ready)
                if attend:
                    row_max(a, 4)
                if front:
                    lo_of(G1, cT_hi, cT_lo, cTh_ready, f + 1, cTl_ready)
                if attend:
                    exp_lo(a, 3)
                if back:
                    lo_of(G0, x2T_hi, x2T_lo, x2h_ready, b + 1, x2l_ready)
                if attend:
                    row_max(a, 5)
                    exp_lo(a, 4)
                    normalise(a, 3)
                    row_max(a, 6)
                    exp_lo(a, 5)
                    row_max(a, 7)
                if back:
                    dve.wait_ge(gt_done, b + 1)
                    lg = G0[:, 0:256].rearrange("p (s t) -> p s t", s=2)[:, :, 0:NE]
                    v.tensor_reduce(r_max[:], lg, AX_X, ALU.max, negate=True).then_inc(rmax_ready, 1)
                    dve.wait_ge(rmax_ready, b + 1)
                    v.tensor_tensor(r_sub[:], lg, r_max[:].unsqueeze(2).broadcast_to([P, 2, NE]), ALU.add
                                    ).then_inc(rsub_ready, 1)
                if attend:
                    exp_lo(a, 6)
                if back:
                    n = 3 * b
                    dve.wait_ge(rexp_ready, b + 1)
                    v.tensor_reduce(r_sum[:], r_exp[:], AX_X, ALU.add).then_inc(prob_step, 1)
                    dve.wait_ge(prob_step, n + 1)
                    v.reciprocal(r_inv[:], r_sum[:]).then_inc(prob_step, 1)
                    dve.wait_ge(prob_step, n + 2)
                    v.tensor_tensor(prob[:], r_exp[:], r_inv[:].unsqueeze(2).broadcast_to([P, 2, NE]),
                                    ALU.mult).then_inc(prob_step, 1)
                    dve.wait_ge(prob_step, n + 3)
                    of_j = prob[:].unsqueeze(2).broadcast_to([P, 2, NE, NE])
                    of_e = prob[:].unsqueeze(3).broadcast_to([P, 2, NE, NE])
                    v.tensor_tensor(cmp_gt[:], of_j, of_e, ALU.is_gt)
                    v.tensor_tensor(cmp_eq[:], of_j, of_e, ALU.is_equal).then_inc(cmp_ready, 1)
                if attend:
                    normalise(a, 5)
                    exp_lo(a, 7)
                if isinstance(i, int) and i == 0:
                    prepare_experts()
                if back:
                    n = 2 * b
                    dve.wait_ge(cmp_step, 2 * b + 2)
                    v.tensor_reduce(rank[:], cmp_gt[:], AX_X, ALU.add).then_inc(rank_step, 1)
                    dve.wait_ge(rank_step, n + 1)
                    v.scalar_tensor_tensor(out=w_tok[:], in0=rank[:], scalar=1.5, in1=prob[:],
                                           op0=ALU.is_lt, op1=ALU.mult).then_inc(rank_step, 1)
                    dve.wait_ge(rank_step, n + 2)
                    accumulate(b, 0)
                if attend:
                    normalise(a, 7)
                if back:
                    for k in range(1, 4):
                        accumulate(b, k)

            run_steps(dve, step)

        @block.gpsimd
        def _(pool):
            g = nc.gpsimd
            g.memset(bias_sel[:], 0.0).then_inc(pool_setup, 1)
            g.memset(ebias[:], 0.0).then_inc(pool_setup, 1)
            pool.wait_ge(pool_setup, 2)
            g.memset(bias_sel[0:3, :], 1.0).then_inc(pool_setup, 1)
            pool.wait_ge(consts_ready, 2)

            def heads(t):
                return t.rearrange("p s (h d) -> p s h d", d=HD)

            def round_to(dst, src):
                return g.tensor_scalar(dst, src, 1.0, 1.0, ALU.mult, ALU.mult)

            def inverse_deviation(rs, ve, step, n):
                g.tensor_tensor(rs[:, 0, :], ve[:, 0, :], half_neg[:], ALU.pow).then_inc(step, 1)
                pool.wait_ge(step, n + 1)
                g.tensor_tensor(rs[:, 1, :], rs[:, 0, :], ve[:, 1, :], ALU.mult).then_inc(step, 1)

            def step(i):
                front, attend, back, combine = stages(i)
                f, b = i, i - 2
                if front:
                    pool.wait_ge(ln1_step, 3 * f + 3)
                    inverse_deviation(rs1, ve1, rs1_step, 2 * f)
                if back:
                    pool.wait_ge(res_loaded, 16 * b + 16)
                    wait(pool, x1_ready, b)
                    g.tensor_tensor(xb[:], x_res[:], bo_row[:].unsqueeze(1).broadcast_to([P, 2, C]), ALU.add
                                    ).then_inc(xb_ready, 1)
                    pool.wait_ge(ln2_step, 3 * b + 3)
                    inverse_deviation(rs2, ve2, rs2_step, 2 * b)
                    wait_alone(pool, y_ready, b)
                    g.tensor_scalar(x1_kept[:], x1[:], 1.0, 1.0, ALU.mult, ALU.mult).then_inc(x1_copied, 1)
                if front:
                    wait_alone(pool, k32_ready, f + 1)
                    round_to(k_round[:], k32[:]).then_inc(k_rounded, 1)
                    pool.wait_ge(k_rounded, 2 * f + 1)
                    g.tensor_tensor(k_rest[:], k32[:], k_round[:].bitcast(F32), ALU.subtract
                                    ).then_inc(k_rounded, 1)
                if back:
                    pool.wait_ge(cmp_ready, b + 1)
                    low = cst[:, C_LOWER:C_LOWER + 64].rearrange("p (e j) -> p e j", e=NE).unsqueeze(1)
                    g.tensor_tensor(cmp_eq[:], cmp_eq[:], low.broadcast_to([P, 2, NE, NE]), ALU.mult
                                    ).then_inc(cmp_step, 1)
                    pool.wait_ge(cmp_step, 2 * b + 1)
                    g.tensor_tensor(cmp_gt[:], cmp_gt[:], cmp_eq[:], ALU.add).then_inc(cmp_step, 1)
                if front:
                    pool.wait_ge(q32_ready, f + 1)
                    wait_alone(pool, s_done, 8 * f)
                    q_in = q32[:, :, :].rearrange("p a (s t) -> p a s t", s=2)
                    round_to(q_hi[:, :, :, :], q_in).then_inc(q_split, 1)
                    pool.wait_ge(q_split, 2 * f + 1)
                    g.tensor_tensor(q_lo[:, :, :, :], q_in, q_hi[:, :, :, :].bitcast(F32), ALU.subtract
                                    ).then_inc(q_split, 1)
                    wait_alone(pool, k_rounded, 2 * f + 2)
                    for dst, src in ((k_hi, k_round[:].bitcast(F32)), (k_lo, k_rest[:])):
                        for r in range(2):
                            for k in range(KC):
                                last = g.tensor_scalar(dst[:, k, :, r, :],
                                                       src[:, k, :].rearrange("p (s t) -> p s t", s=2),
                                                       parity[r], 1.0, ALU.mult, ALU.mult)
                    last.then_inc(k_split, 1)
                    n = 6 * f
                    pool.wait_ge(v_raw_ready, f + 1)
                    g.tensor_tensor(v32[:], v_raw[:], bv_row[:].unsqueeze(1).broadcast_to([P, 2, C]), ALU.add
                                    ).then_inc(v_split, 1)
                    pool.wait_ge(v_split, n + 1)
                    wait_alone(pool, pv_done, 8 * f)
                    round_to(v_part[:, :, :, 0:HD], heads(v32[:])).then_inc(v_split, 1)
                    pool.wait_ge(v_split, n + 2)
                    g.tensor_tensor(heads(v_rest[:]), heads(v32[:]), v_part[:, :, :, 0:HD], ALU.subtract
                                    ).then_inc(v_split, 1)
                    wait_alone(pool, v_split, n + 3)
                    round_to(v_part[:, :, :, HD:2 * HD], heads(v_rest[:])).then_inc(v_split, 1)
                    pool.wait_ge(v_split, n + 4)
                    g.tensor_tensor(heads(v_rest[:]), heads(v_rest[:]), v_part[:, :, :, HD:2 * HD], ALU.subtract
                                    ).then_inc(v_split, 1)
                    wait_alone(pool, v_split, n + 5)
                    round_to(v_part[:, :, :, 2 * HD:3 * HD], heads(v_rest[:])).then_inc(v_split, 1)

            run_steps(pool, step)


_INS = ['x', 'ctx_1024', 'g_xattn', 'g_ffn', 'L0_xattn_wq', 'L0_xattn_bq', 'L0_xattn_wk', 'L0_xattn_bk',
        'L0_xattn_wv', 'L0_xattn_bv', 'L0_xattn_wo', 'L0_xattn_bo', 'L0_ffn_gate_w', 'L0_ffn_expert_w',
        'L0_ffn_expert_b', 'L0_ffn_combine_w']
_OUTS = [((64, 128, 256), 'float32')]


def kernel(**inputs):
    import numpy as _np
    import concourse.bacc as _bacc
    from concourse import mybir as _mybir
    from concourse.bass_utils import run_bass_kernel_spmd as _run

    nc = _bacc.Bacc("TRN2", target_bir_lowering=False, num_devices=1)
    arrays, args = {}, []
    for name in _INS:
        a = _np.ascontiguousarray(inputs[name])
        arrays[f"in_{name}_dram"] = a
        args.append(nc.dram_tensor(f"in_{name}_dram", a.shape, _mybir.dt.from_np(a.dtype), kind="ExternalInput").ap())
    c = _np.zeros((P, C_COLS), _np.float32)
    c[:, C_IDENT:C_IDENT + P] = _np.eye(P)
    c[:, C_CAUSAL:C_CAUSAL + P] = _np.triu(_np.full((P, P), -3.0e38), 1)
    c[:, C_PARITY] = _np.arange(P) // 16 % 2 == 0
    c[:, C_PARITY + 1] = _np.arange(P) // 16 % 2 == 1
    c[:, C_LOWER:C_LOWER + 64] = _np.tril(_np.ones((8, 8)), -1).reshape(1, 64)
    arrays["consts_dram"] = c
    args.append(nc.dram_tensor("consts_dram", c.shape, _mybir.dt.float32, kind="ExternalInput").ap())
    for i, (shape, dtype) in enumerate(_OUTS):
        dt = _mybir.dt.from_np(_np.dtype(dtype))
        args.append(nc.dram_tensor(f"out_{i}_dram", shape, dt, kind="ExternalOutput").ap())
    flamingo_block(nc, *args)
    r = _run(nc, [arrays], core_ids=[0])
    got = tuple(r.results[0][f"out_{i}_dram"] for i in range(len(_OUTS)))
    return got[0]
```

```python
from contextlib import ExitStack

import concourse.bass as bass
from concourse import mybir

P = 128
ALU = mybir.AluOpType
ACT = mybir.ActivationFunctionType
AX_X = mybir.AxisListType.X
F32 = mybir.dt.float32
F32R = mybir.dt.float32r
BF16 = mybir.dt.bfloat16
FP16 = mybir.dt.float16

C_IDENT = 0
C_CAUSAL = 128
C_PARITY = 256
C_LOWER = 258
C_COLS = 258 + 64


def flamingo_block(
    nc: bass.Bass,
    x: bass.AP,
    ctx_1024: bass.AP,
    g_xattn: bass.AP,
    g_ffn: bass.AP,
    L0_xattn_wq: bass.AP,
    L0_xattn_bq: bass.AP,
    L0_xattn_wk: bass.AP,
    L0_xattn_bk: bass.AP,
    L0_xattn_wv: bass.AP,
    L0_xattn_bv: bass.AP,
    L0_xattn_wo: bass.AP,
    L0_xattn_bo: bass.AP,
    L0_ffn_gate_w: bass.AP,
    L0_ffn_expert_w: bass.AP,
    L0_ffn_expert_b: bass.AP,
    L0_ffn_combine_w: bass.AP,
    consts: bass.AP,
    out: bass.AP,
):
    NSEQ, T, C = x.shape
    NPAIR = NSEQ // 2
    KC = C // P
    HD = 16
    H = C // HD
    NE = L0_ffn_expert_w.shape[0]
    VC = 3 * HD + 1
    SU = 8
    EU = 8
    SCALE = float(HD) ** -0.5
    EPS = 1e-5
    assert T == P and C == 2 * P and H == 16 and NE == 8

    with ExitStack() as ctx:
        def sb(name, shape, dt=F32):
            return ctx.enter_context(nc.sbuf_tensor(name, shape, dt))

        def sem(name):
            return ctx.enter_context(nc.semaphore(name))

        cst = sb("cst", [P, C_COLS])
        ident = cst[:, C_IDENT:C_IDENT + P]
        causal = cst[:, C_CAUSAL:C_CAUSAL + P]
        parity = [cst[:, C_PARITY + j:C_PARITY + j + 1] for j in range(2)]
        half_neg = sb("half_neg", [P, 2])
        bias_sel = sb("bias_sel", [P, P], BF16)
        ebias = sb("ebias", [P, NE * C], BF16)
        eb_nat = sb("eb_nat", [16, P])
        eb_rest = sb("eb_rest", [16, 2, P])
        eb_part = sb("eb_part", [16, 3, P], BF16)
        gates = sb("gates", [P, 4])
        g_raw = sb("g_raw", [P, 2])
        bq_col = sb("bq_col", [P, KC])
        bk_col = sb("bk_col", [P, KC])
        bv_row = sb("bv_row", [P, C])
        bo_row = sb("bo_row", [P, C])
        w_nat = sb("w_nat", [P, 6 + NE, KC, C])
        w_hi = sb("w_hi", [P, 5, KC, C], F32R)
        w_lo = sb("w_lo", [P, 5, KC, C], F32R)
        gw_hi = sb("gw_hi", [P, KC, P], F32R)
        gw_lo = sb("gw_lo", [P, KC, P], F32R)
        ew_hi = sb("ew_hi", [P, KC, NE, C], F32R)
        ew_lo = sb("ew_lo", [P, KC, NE, C], F32R)

        x_in = sb("x_in", [P, 2, C])
        c_in = sb("c_in", [P, 2, C])
        x_res = sb("x_res", [P, 2, C])
        xb = sb("xb", [P, 2, C])
        st1 = sb("st1", [P, 2, 6])
        mv1 = sb("mv1", [P, 2, 2])
        ve1 = sb("ve1", [P, 2, 2])
        rs1 = sb("rs1", [P, 2, 2])
        xn = sb("xn", [P, 2, C])
        xT_hi = sb("xT_hi", [P, KC, 2, P], F32R)
        xT_lo = sb("xT_lo", [P, KC, 2, P], F32R)
        cT_hi = sb("cT_hi", [P, KC, 2, P], F32R)
        cT_lo = sb("cT_lo", [P, KC, 2, P], F32R)
        q32 = sb("q32", [P, KC, 2 * P])
        k32 = sb("k32", [P, KC, 2 * P])
        k_round = sb("k_round", [P, KC, 2 * P], F32R)
        k_rest = sb("k_rest", [P, KC, 2 * P])
        q_hi = sb("q_hi", [P, KC, 2, P], F32R)
        q_lo = sb("q_lo", [P, KC, 2, P], F32R)
        k_hi = sb("k_hi", [P, KC, 2, 2, P], F32R)
        k_lo = sb("k_lo", [P, KC, 2, 2, P], F32R)
        v_raw = sb("v_raw", [P, 2, C])
        v32 = sb("v32", [P, 2, C])
        v_rest = sb("v_rest", [P, 2, C])
        v_part = sb("v_part", [P, 2, H, VC], BF16)
        neg_s = sb("neg_s", [P, 2, 4, P])
        neg_max = sb("neg_max", [P, SU, 4])
        e_q = sb("e_q", [P, 4, 4, P])
        e_hi = sb("e_hi", [P, 2, 4, P], FP16)
        e_lo = sb("e_lo", [P, 2, 4, P], FP16)
        inv_sum = sb("inv_sum", [P, 2, 4])
        o_sum = sb("o_sum", [P, 2, 4, HD])
        o_n = sb("o_n", [P, 2, 2, 2, 4, HD])
        oT_hi = sb("oT_hi", [P, KC, 2, P], F32R)
        oT_lo = sb("oT_lo", [P, KC, 2, P], F32R)
        x1 = sb("x1", [P, 2, C])
        x1_kept = sb("x1_kept", [P, 2, C])
        st2 = sb("st2", [P, 2, 6])
        mv2 = sb("mv2", [P, 2, 2])
        ve2 = sb("ve2", [P, 2, 2])
        rs2 = sb("rs2", [P, 2, 2])
        xn2 = sb("xn2", [P, 2, C])
        x2T_hi = sb("x2T_hi", [P, KC, 2, P], F32R)
        x2T_lo = sb("x2T_lo", [P, KC, 2, P], F32R)
        lgT = sb("lgT", [P, 2, P])
        r_max = sb("r_max", [P, 2])
        r_sub = sb("r_sub", [P, 2, NE])
        r_exp = sb("r_exp", [P, 2, NE])
        r_sum = sb("r_sum", [P, 2])
        r_inv = sb("r_inv", [P, 2])
        prob = sb("prob", [P, 2, NE])
        cmp_gt = sb("cmp_gt", [P, 2, NE, NE])
        cmp_eq = sb("cmp_eq", [P, 2, NE, NE])
        rank = sb("rank", [P, 2, NE])
        w_tok = sb("w_tok", [P, 2, NE])
        act_e = sb("act_e", [P, 4, 2, C])
        mix = sb("mix", [P, 2, C])
        mT_hi = sb("mT_hi", [P, KC, 2, P], F32R)
        mT_lo = sb("mT_lo", [P, KC, 2, P], F32R)
        y = sb("y", [P, 2, C])
        table = sb("table", [P, 2])

        banks = [ctx.enter_context(nc.psum_tensor(f"bank{i}", [P, 512], F32)) for i in range(8)]
        S = [banks[0], banks[1]]
        TB = banks[2]
        OB = banks[3]
        E = [banks[4], banks[5]]
        G0 = banks[6]
        G1 = banks[7]

        def quad(b):
            return b[:, :].rearrange("p (a s t) -> p a s t", a=2, s=2)

        ld_first = sem("ld_first")
        ld_second = sem("ld_second")
        ld_rest = sem("ld_rest")
        ld_experts = sem("ld_experts")
        w_cleared = sem("w_cleared")
        gates_ready = sem("gates_ready")
        w_transposed = sem("w_transposed")
        w_hi_ready = sem("w_hi_ready")
        w_lo_ready = sem("w_lo_ready")
        ew_transposed = sem("ew_transposed")
        ew_hi_ready = sem("ew_hi_ready")
        ew_lo_ready = sem("ew_lo_ready")
        consts_ready = sem("consts_ready")
        pool_setup = sem("pool_setup")
        eb_step = sem("eb_step")
        ebias_ready = sem("ebias_ready")

        x_loaded = sem("x_loaded")
        c_loaded = sem("c_loaded")
        res_loaded = sem("res_loaded")
        y_stored = sem("y_stored")
        ln1_step = sem("ln1_step")
        rs1_step = sem("rs1_step")
        xn_ready = sem("xn_ready")
        xt_done = sem("xt_done")
        xTh_ready = sem("xTh_ready")
        xTl_ready = sem("xTl_ready")
        ct_done = sem("ct_done")
        cTh_ready = sem("cTh_ready")
        cTl_ready = sem("cTl_ready")
        q_done = sem("q_done")
        q32_ready = sem("q32_ready")
        q_split = sem("q_split")
        k_done = sem("k_done")
        k32_ready = sem("k32_ready")
        k_rounded = sem("k_rounded")
        k_split = sem("k_split")
        v_done = sem("v_done")
        v_raw_ready = sem("v_raw_ready")
        v_split = sem("v_split")
        s_done = sem("s_done")
        max_ready = sem("max_ready")
        exp_ready = sem("exp_ready")
        t_done = sem("t_done")
        eh_ready = sem("eh_ready")
        el_ready = sem("el_ready")
        pv_done = sem("pv_done")
        norm_step = sem("norm_step")
        norm_ready = sem("norm_ready")
        ot_done = sem("ot_done")
        oTh_ready = sem("oTh_ready")
        oTl_ready = sem("oTl_ready")
        p_done = sem("p_done")
        xb_ready = sem("xb_ready")
        x1_ready = sem("x1_ready")
        x1_copied = sem("x1_copied")
        ln2_step = sem("ln2_step")
        rs2_step = sem("rs2_step")
        xn2_ready = sem("xn2_ready")
        x2t_done = sem("x2t_done")
        x2h_ready = sem("x2h_ready")
        x2l_ready = sem("x2l_ready")
        gl_done = sem("gl_done")
        lgT_ready = sem("lgT_ready")
        gt_done = sem("gt_done")
        rmax_ready = sem("rmax_ready")
        rsub_ready = sem("rsub_ready")
        rexp_ready = sem("rexp_ready")
        prob_step = sem("prob_step")
        cmp_ready = sem("cmp_ready")
        cmp_step = sem("cmp_step")
        rank_step = sem("rank_step")
        e_done = sem("e_done")
        silu_ready = sem("silu_ready")
        acc_step = sem("acc_step")
        mt_done = sem("mt_done")
        mTh_ready = sem("mTh_ready")
        mTl_ready = sem("mTl_ready")
        comb_done = sem("comb_done")
        y_ready = sem("y_ready")

        def wait(eng, s, value):
            if not (isinstance(value, int) and value <= 0):
                eng.wait_ge(s, value)

        def wait_alone(eng, s, value):
            wait(eng, s, value)
            eng.nop(nofuse=True)

        def stages(i):
            pairs = [i - k for k in range(5)]
            on = [True if not isinstance(p, int) else 0 <= p < NPAIR for p in pairs]
            return *pairs, on

        FILL = 5

        def run_steps(eng, step):
            for i in range(1, FILL):
                step(i)
            with eng.Fori(FILL, NPAIR) as i:
                step(i)
            for i in range(NPAIR, NPAIR + 4):
                step(i)

        attn_w = [L0_xattn_wq, L0_xattn_wk, L0_xattn_wv, L0_xattn_wo, L0_ffn_combine_w]
        scale_of = [3, 0, 0, 1, 2]
        WQ, WK, WV, WO, WC = range(5)
        x_pairs = x.rearrange("(i s) p c -> i p s c", s=2)
        c_pairs = ctx_1024.rearrange("(i s) p c -> i p s c", s=2)
        out_pairs = out.rearrange("(i s) p c -> i p s c", s=2)
        N_FIRST = 16 * (1 + 2 + len(attn_w))
        N_SECOND = 16 * (1 + 4)

        block = ctx.enter_context(nc.Block())

        @block.sync
        def _(sp):
            sp.dma_start(x_in[:], x_pairs[0]).then_inc(x_loaded, 16)
            sp.dma_start(cst[:], consts).then_inc(ld_first, 16)
            for j, g in enumerate((g_xattn, g_ffn)):
                sp.dma_start(g_raw[:, j:j + 1], g.rearrange("(o n) -> o n", o=1).broadcast_to([P, 1])
                             ).then_inc(ld_first, 16)
            for j, w in enumerate(attn_w):
                sp.dma_start(w_nat[:, j], w.rearrange("(a p) c -> p a c", p=P)).then_inc(ld_first, 16)
            sp.dma_start(c_in[:], c_pairs[0]).then_inc(c_loaded, 16)
            sp.wait_ge(w_cleared, 1)
            sp.dma_start(w_nat[0:NE, 5, 0, :], L0_ffn_gate_w).then_inc(ld_second, 16)
            for col, b in ((bq_col, L0_xattn_bq), (bk_col, L0_xattn_bk)):
                sp.dma_start(col[:], b.rearrange("(a p) -> p a", p=P), allow_slow_non_contiguous=True).then_inc(ld_second, 16)
            for row, b in ((bv_row, L0_xattn_bv), (bo_row, L0_xattn_bo)):
                sp.dma_start(row[:], b.rearrange("(o n) -> o n", o=1).broadcast_to([P, C])
                             ).then_inc(ld_second, 16)
            sp.dma_start(eb_nat[:], L0_ffn_expert_b.rearrange("e (h c) -> (e h) c", c=P)).then_inc(ld_rest, 16)
            for e in range(NE):
                sp.dma_start(w_nat[:, 6 + e], L0_ffn_expert_w[e].rearrange("(a p) c -> p a c", p=P)
                             ).then_inc(ld_experts, 16)

            def step(i):
                p0, p1, p2, p3, p4, on = stages(i)
                if on[0]:
                    wait(sp, xn_ready, p0)
                    sp.dma_start(x_in[:], x_pairs[p0]).then_inc(x_loaded, 16)
                if on[2]:
                    wait(sp, xb_ready, p2)
                    sp.dma_start(x_res[:], x_pairs[p2]).then_inc(res_loaded, 16)
                if on[4]:
                    sp.wait_ge(y_ready, p4 + 1)
                    sp.dma_start(out_pairs[p4], y[:]).then_inc(y_stored, 16)
                if on[0]:
                    wait(sp, ct_done, p0)
                    sp.dma_start(c_in[:], c_pairs[p0]).then_inc(c_loaded, 16)
                if isinstance(i, int) and i == 2:
                    sp.wait_ge(eb_step, 5)
                    sp.wait_ge(pool_setup, 2)
                    for k in range(3):
                        sp.dma_start(ebias[k:k + 1, :].rearrange("o (h c) -> o h c", c=P),
                                     eb_part[:, k, :]).then_inc(ebias_ready, 16)

            run_steps(sp, step)
            sp.wait_ge(y_stored, 16 * NPAIR)

        @block.tensor
        def _(pe):
            mm = nc.tensor.matmul

            def transpose4(bank, src, done):
                for s in range(2):
                    for a in range(KC):
                        last = nc.tensor.transpose(quad(bank)[:, a, s, :], src[:, s, a * P:(a + 1) * P], ident)
                last.then_inc(done, 1)

            def project_T(bank, w, hi, lo, done):
                for a in range(KC):
                    terms = [(l[:, w, kc, a * P:(a + 1) * P], r[:, kc, :, :])
                             for l, r in ((w_hi, hi), (w_hi, lo), (w_lo, hi)) for kc in range(KC)]
                    for n, (l, r) in enumerate(terms):
                        last = mm(bank[:, a * 256:(a + 1) * 256], l, r, start=n == 0, stop=n == len(terms) - 1)
                last.then_inc(done, 1)

            def project(bank, w, hi, lo, done):
                for s in range(2):
                    terms = [(l[:, kc, s, :], r[:, w, kc, :])
                             for l, r in ((hi, w_hi), (hi, w_lo), (lo, w_hi)) for kc in range(KC)]
                    for n, (l, r) in enumerate(terms):
                        last = mm(bank[:, s * 256:(s + 1) * 256], l, r, start=n == 0, stop=n == len(terms) - 1)
                last.then_inc(done, 1)

            def scores(p, u):
                s, g = divmod(u, 4)
                rows = slice(32 * g, 32 * g + 32)
                bank = S[u % 2]
                if u == 0:
                    pe.wait_ge(q_split, 2 * p + 2)
                    pe.wait_ge(k_split, p + 1)
                wait(pe, max_ready, 8 * p + u - 1)
                for a in range(KC):
                    for n, (l, r) in enumerate(((q_hi, k_hi), (q_lo, k_hi), (q_hi, k_lo))):
                        last = mm(bank[:, a * 256:(a + 1) * 256], l[rows, a, s, :],
                                  r[rows, a, s, :, :], start=n == 0, stop=n == 2)
                last.then_inc(s_done, 1)

            def transposed_exp(p, u):
                pe.wait_ge(exp_ready, 8 * p + u + 1)
                wait(pe, el_ready, 8 * p + u)
                for j in range(4):
                    last = nc.tensor.transpose(TB[:, j * P:(j + 1) * P], e_q[:, u % 4, j, :], ident)
                last.then_inc(t_done, 1)
                if isinstance(p, int) and p == 0:
                    if u == 0:
                        pe.wait_ge(ld_experts, 16 * NE)
                    if u >= 2:
                        pe.wait_ge(ew_lo_ready, u - 1)
                    prepare(E[u % 2], 6 + u, ew_transposed)

            def times_v(p, u):
                s, g = divmod(u, 4)
                if u == 0:
                    pe.wait_ge(v_split, 6 * p + 6)
                pe.wait_ge(el_ready, 8 * p + u + 1)
                if u % 2 == 0:
                    wait(pe, norm_ready, 4 * p + u // 2)
                for j in range(4):
                    a, odd = divmod(j, 2)
                    c0 = (4 * a + 2 * (u % 2) + odd) * VC
                    v = v_part[:, s, 8 * a + 2 * g + odd, :]
                    mm(OB[:, c0:c0 + VC], e_hi[:, u % 2, j, :], v, start=True, stop=False)
                    last = mm(OB[:, c0:c0 + VC], e_lo[:, u % 2, j, :], v, start=False, stop=True)
                last.then_inc(pv_done, 1)

            def expert_unit(p, e):
                f, s = divmod(e, 2)
                bank = E[e % 2]
                if e == 0:
                    pe.wait_ge(x2l_ready, p + 1)
                    if isinstance(p, int) and p == 0:
                        pe.wait_ge(ew_lo_ready, NE)
                        pe.wait_ge(pool_setup, 3)
                        pe.wait_ge(ebias_ready, 48)
                wait(pe, silu_ready, 8 * p + e - 1)
                mm(bank[:, :], bias_sel[:], ebias[:, f * 512:(f + 1) * 512], start=True, stop=False)
                terms = [(l[:, kc, s, :], r[:, kc, 2 * f:2 * f + 2, :])
                         for kc in range(KC) for l, r in ((x2T_hi, ew_hi), (x2T_hi, ew_lo), (x2T_lo, ew_hi))]
                for n, (l, r) in enumerate(terms):
                    last = mm(bank[:, :], l, r, start=False, stop=n == len(terms) - 1)
                last.then_inc(e_done, 1)

            def prepare(bank, m, done):
                for a in range(1 if m == 5 else KC):
                    for kc in range(KC):
                        o = bank[:, kc * C + a * P:kc * C + (a + 1) * P]
                        last = nc.tensor.transpose(o, w_nat[:, m, a, kc * P:(kc + 1) * P], ident)
                last.then_inc(done, 1)

            pe.wait_ge(ld_first, N_FIRST)
            for m in range(6):
                if m == 5:
                    pe.wait_ge(ld_second, N_SECOND)
                prepare(banks[m], m, w_transposed)

            def transpose_attention(p):
                pe.wait_ge(norm_ready, 4 * p + 4)
                transpose4(G0, o_n[:].rearrange("p s a b h d -> p s (a b h d)"), ot_done)

            def output_projection(p):
                pe.wait_ge(oTl_ready, p + 1)
                project(G0, WO, oT_hi, oT_lo, p_done)

            def transpose_mixture(p):
                pe.wait_ge(acc_step, 16 * p + 16)
                transpose4(G1, mix, mt_done)

            def combination(p):
                pe.wait_ge(mTl_ready, p + 1)
                project(G1, WC, mT_hi, mT_lo, comb_done)

            def transpose_context(p):
                pe.wait_ge(c_loaded, 16 * p + 16)
                transpose4(G0, c_in, ct_done)

            def keys(p):
                if isinstance(p, int) and p == 0:
                    pe.wait_ge(w_lo_ready, 6)
                pe.wait_ge(cTl_ready, p + 1)
                project_T(G0, WK, cT_hi, cT_lo, k_done)

            def values(p):
                pe.wait_ge(cTl_ready, p + 1)
                project(G0, WV, cT_hi, cT_lo, v_done)

            def transpose_xn(p):
                pe.wait_ge(xn_ready, p + 1)
                transpose4(G0, xn, xt_done)

            def queries(p):
                pe.wait_ge(xTl_ready, p + 1)
                project_T(G0, WQ, xT_hi, xT_lo, q_done)

            def transpose_xn2(p):
                pe.wait_ge(xn2_ready, p + 1)
                transpose4(G1, xn2, x2t_done)

            def router_logits(p):
                pe.wait_ge(x2l_ready, p + 1)
                for n, (l, r) in enumerate(((gw_hi, x2T_hi), (gw_hi, x2T_lo), (gw_lo, x2T_hi))):
                    for kc in range(KC):
                        last = mm(G1[:, 0:256], l[:, kc, :], r[:, kc, :, :],
                                  start=n == 0 and kc == 0, stop=n == 2 and kc == 1)
                last.then_inc(gl_done, 1)

            def transpose_logits(p):
                pe.wait_ge(lgT_ready, p + 1)
                for s in range(2):
                    last = nc.tensor.transpose(G1[:, s * P:(s + 1) * P], lgT[:, s, :], ident)
                last.then_inc(gt_done, 1)

            def turn(*readers):
                for sem, value in readers:
                    if not isinstance(value, int) or 1 <= value <= NPAIR:
                        pe.wait_ge(sem, value)
                        return

            def step(i):
                p0, p1, p2, p3, p4, on = stages(i)
                if on[2]:
                    scores(p2, 0)
                if on[3]:
                    times_v(p3, 4)
                    transposed_exp(p3, 6)
                    times_v(p3, 5)
                if on[4]:
                    expert_unit(p4, 2)
                    expert_unit(p4, 3)
                if on[3]:
                    transposed_exp(p3, 7)
                    times_v(p3, 6)
                if on[4]:
                    expert_unit(p4, 4)
                    expert_unit(p4, 5)
                if on[3]:
                    times_v(p3, 7)
                if on[4]:
                    expert_unit(p4, 6)
                if on[3]:
                    turn((v_raw_ready, p1), (x1_ready, p3))
                    transpose_attention(p3)
                if on[4]:
                    expert_unit(p4, 7)
                if on[2]:
                    scores(p2, 1)
                if on[3]:
                    pe.wait_ge(oTl_ready, p3 + 1)
                    output_projection(p3)
                if on[2]:
                    scores(p2, 2)
                if on[4]:
                    pe.wait_ge(rsub_ready, p3)
                    transpose_mixture(p4)
                if on[1]:
                    turn((x1_ready, p3 + 1), (v_raw_ready, p1))
                    transpose_context(p1)
                if on[2]:
                    transposed_exp(p2, 0)
                    scores(p2, 3)
                    scores(p2, 4)
                if on[1]:
                    pe.wait_ge(cTl_ready, p1 + 1)
                    keys(p1)
                if on[2]:
                    transposed_exp(p2, 1)
                if on[4]:
                    pe.wait_ge(mTl_ready, p4 + 1)
                    combination(p4)
                if on[2]:
                    times_v(p2, 0)
                if on[1]:
                    pe.wait_ge(k32_ready, p1 + 1)
                    transpose_xn(p1)
                if on[2]:
                    scores(p2, 5)
                    transposed_exp(p2, 2)
                    times_v(p2, 1)
                    scores(p2, 6)
                if on[1]:
                    pe.wait_ge(xTl_ready, p1 + 1)
                    queries(p1)
                if on[2]:
                    scores(p2, 7)
                    transposed_exp(p2, 3)
                if on[3]:
                    turn((y_ready, p4 + 1))
                    transpose_xn2(p3)
                if on[2]:
                    times_v(p2, 2)
                if on[1]:
                    pe.wait_ge(q32_ready, p1 + 1)
                    values(p1)
                if on[2]:
                    transposed_exp(p2, 4)
                    times_v(p2, 3)
                if on[3]:
                    pe.wait_ge(x2l_ready, p3 + 1)
                    router_logits(p3)
                    expert_unit(p3, 0)
                if on[2]:
                    transposed_exp(p2, 5)
                if on[3]:
                    pe.wait_ge(lgT_ready, p3 + 1)
                    transpose_logits(p3)
                    expert_unit(p3, 1)

            run_steps(pe, step)

        @block.scalar
        def _(act):
            def hi_of(bank, dst, ready):
                nc.scalar.activation(dst[:, :, :, :], quad(bank), ACT.Copy).then_inc(ready, 1)

            def prepare_weights():
                act.wait_ge(ld_first, N_FIRST)
                nc.scalar.activation(gates[:, 1:3], g_raw[:], ACT.Tanh).then_inc(gates_ready, 1)
                act.wait_ge(gates_ready, 2)
                for m in range(6):
                    act.wait_ge(w_transposed, m + 1)
                    src = banks[m][:, :].rearrange("p (k c) -> p k c", k=KC)
                    dst, g = (w_hi[:, m], scale_of[m]) if m < 5 else (gw_hi[:], 0)
                    if m == 5:
                        src = src[:, :, 0:P]
                    nc.scalar.activation(dst, src, ACT.Copy, scale=gates[:, g:g + 1]).then_inc(w_hi_ready, 1)

            def normed(dst, src, rs, ready):
                for s in range(2):
                    last = nc.scalar.activation(dst[:, s, :], src[:, s, :], ACT.Identity,
                                                scale=rs[:, 0, s:s + 1], bias=rs[:, 1, s:s + 1])
                last.then_inc(ready, 1)

            def exps(p, u):
                act.wait_ge(max_ready, 8 * p + u + 1)
                wait(act, t_done, 8 * p + u - 3)
                for j in range(4):
                    last = nc.scalar.activation(e_q[:, u % 4, j, :], neg_s[:, u % 2, j, :], ACT.Exp,
                                                bias=neg_max[:, u, j:j + 1], scale=-1.0)
                last.then_inc(exp_ready, 1)

            def exp_hi(p, u):
                act.wait_ge(t_done, 8 * p + u + 1)
                wait(act, pv_done, 8 * p + u - 1)
                nc.scalar.activation(e_hi[:, u % 2, :, :], TB[:, :].rearrange("p (j t) -> p j t", j=4),
                                     ACT.Copy).then_inc(eh_ready, 1)
                if isinstance(p, int) and p == 0:
                    act.wait_ge(ew_transposed, u + 1)
                    nc.scalar.activation(ew_hi[:, :, u, :], E[u % 2][:, :].rearrange("p (k c) -> p k c", k=KC),
                                         ACT.Copy).then_inc(ew_hi_ready, 1)

            def silu(p, e):
                act.wait_ge(e_done, 8 * p + e + 1)
                wait(act, acc_step, 16 * p + 4 * (e // 2 - 1))
                nc.scalar.activation(act_e[:, e % 4, :, :], E[e % 2][:, :].rearrange("p (f c) -> p f c", f=2),
                                     ACT.Silu).then_inc(silu_ready, 1)

            def attention_hi(p):
                act.wait_ge(ot_done, p + 1)
                wait(act, p_done, p)
                hi_of(G0, oT_hi, oTh_ready)

            def mixture_hi(p):
                act.wait_ge(mt_done, p + 1)
                wait(act, comb_done, p)
                hi_of(G1, mT_hi, mTh_ready)

            def context_hi(p):
                act.wait_ge(ct_done, p + 1)
                wait(act, k_done, p)
                wait(act, v_done, p)
                hi_of(G0, cT_hi, cTh_ready)

            def xn_hi(p):
                act.wait_ge(xt_done, p + 1)
                wait(act, q_done, p)
                hi_of(G0, xT_hi, xTh_ready)

            def xn2_hi(p):
                act.wait_ge(x2t_done, p + 1)
                wait(act, gl_done, p)
                wait(act, e_done, 8 * p)
                hi_of(G1, x2T_hi, x2h_ready)

            def norm_1(p):
                act.wait_ge(rs1_step, 3 * p + 3)
                wait(act, xt_done, p)
                normed(xn, x_in, rs1, xn_ready)

            def norm_2(p):
                act.wait_ge(rs2_step, 3 * p + 3)
                wait(act, x2t_done, p)
                normed(xn2, x1, rs2, xn2_ready)

            def keys_out(p):
                act.wait_ge(k_done, p + 1)
                if isinstance(p, int) and p == 0:
                    act.wait_ge(consts_ready, 2)
                wait(act, k_rounded, 2 * p)
                for k in range(KC):
                    last = nc.scalar.activation(k32[:, k, :], G0[:, k * 256:(k + 1) * 256], ACT.Identity,
                                                bias=bk_col[:, k:k + 1])
                last.then_inc(k32_ready, 1)

            def queries_out(p):
                act.wait_ge(q_done, p + 1)
                wait(act, q_split, 2 * p)
                for k in range(KC):
                    last = nc.scalar.activation(q32[:, k, :], G0[:, k * 256:(k + 1) * 256], ACT.Identity,
                                                bias=bq_col[:, k:k + 1])
                last.then_inc(q32_ready, 1)

            def values_out(p):
                act.wait_ge(v_done, p + 1)
                wait(act, v_split, 6 * p - 5)
                nc.scalar.activation(v_raw[:], G0[:, :].rearrange("p (s c) -> p s c", s=2), ACT.Copy
                                     ).then_inc(v_raw_ready, 1)

            def logits_out(p):
                act.wait_ge(gl_done, p + 1)
                wait(act, gt_done, p)
                nc.scalar.activation(lgT[:], G1[:, 0:256].rearrange("p (s t) -> p s t", s=2),
                                     ACT.Copy).then_inc(lgT_ready, 1)

            def router_exp(p):
                act.wait_ge(rsub_ready, p + 1)
                nc.scalar.activation(r_exp[:], r_sub[:], ACT.Exp).then_inc(rexp_ready, 1)

            def fetch_silu(p):
                nc.scalar.activation(table[:, 1:2], table[:, 0:1], ACT.Silu)

            def fetch_exp(p):
                nc.scalar.activation(table[:, 1:2], table[:, 0:1], ACT.Exp)

            def step(i):
                p0, p1, p2, p3, p4, on = stages(i)
                if on[2]:
                    exps(p2, 0)
                if on[4]:
                    mixture_hi(p4)
                if on[1]:
                    context_hi(p1)
                if on[2]:
                    exp_hi(p2, 0)
                    exps(p2, 1)
                    exps(p2, 2)
                if on[1]:
                    keys_out(p1)
                if on[2]:
                    exp_hi(p2, 1)
                    exps(p2, 3)
                if on[1]:
                    xn_hi(p1)
                if on[2]:
                    exp_hi(p2, 2)
                    exps(p2, 4)
                if on[3]:
                    norm_2(p3)
                if on[1]:
                    queries_out(p1)
                if on[2]:
                    exp_hi(p2, 3)
                if on[3]:
                    xn2_hi(p3)
                if on[2]:
                    exps(p2, 5)
                    exp_hi(p2, 4)
                    exps(p2, 6)
                if on[3]:
                    logits_out(p3)
                if on[2]:
                    exps(p2, 7)
                    exp_hi(p2, 5)
                if on[3]:
                    router_exp(p3)
                    fetch_silu(p3)
                    silu(p3, 0)
                if on[1]:
                    values_out(p1)
                if on[3]:
                    silu(p3, 1)
                if on[2]:
                    exp_hi(p2, 6)
                if on[0]:
                    norm_1(p0)
                if on[3]:
                    silu(p3, 2)
                if on[2]:
                    exp_hi(p2, 7)
                if on[3]:
                    silu(p3, 3)
                    silu(p3, 4)
                    silu(p3, 5)
                if on[2]:
                    attention_hi(p2)
                if on[3]:
                    silu(p3, 6)
                    silu(p3, 7)
                    fetch_exp(p3)

            step(0)
            prepare_weights()
            run_steps(act, step)

        @block.vector
        def _(dve):
            v = nc.vector

            def lo_of(bank, hi, lo, hi_ready, value, ready):
                dve.wait_ge(hi_ready, value)
                v.tensor_tensor(lo[:, :, :, :], quad(bank), hi[:, :, :, :].bitcast(F32), ALU.subtract
                                ).then_inc(ready, 1)

            v.memset(w_nat[:, 5], 0.0).then_inc(w_cleared, 1)
            v.memset(gates[:, 0:1], 1.0)
            v.memset(table[:], 0.0)
            v.memset(v_part[:, :, :, VC - 1:VC], 1.0)
            v.memset(gates[:, 3:4], SCALE).then_inc(gates_ready, 1)
            def prepare_weights():
                dve.wait_ge(gates_ready, 2)
                for m in range(6):
                    dve.wait_ge(w_hi_ready, m + 1)
                    src = banks[m][:, :].rearrange("p (k c) -> p k c", k=KC)
                    hi, lo, g = (w_hi[:, m], w_lo[:, m], scale_of[m]) if m < 5 else (gw_hi[:], gw_lo[:], 0)
                    if m == 5:
                        src = src[:, :, 0:P]
                    v.scalar_tensor_tensor(out=lo, in0=src, scalar=gates[:, g:g + 1], in1=hi.bitcast(F32),
                                           op0=ALU.mult, op1=ALU.subtract).then_inc(w_lo_ready, 1)
                dve.wait_ge(ld_second, N_SECOND)
                v.tensor_scalar(bq_col[:], bq_col[:], SCALE, None, ALU.mult)
                v.tensor_scalar(bo_row[:], bo_row[:], gates[:, 1:2], None, ALU.mult).then_inc(consts_ready, 2)

            def split_expert_bias():
                dve.wait_ge(ld_rest, 16)
                v.tensor_copy(eb_part[:, 0, :], eb_nat[:]).then_inc(eb_step, 1)
                dve.wait_ge(eb_step, 1)
                v.tensor_tensor(eb_rest[:, 0, :], eb_nat[:], eb_part[:, 0, :], ALU.subtract).then_inc(eb_step, 1)
                dve.wait_ge(eb_step, 2)
                v.tensor_copy(eb_part[:, 1, :], eb_rest[:, 0, :]).then_inc(eb_step, 1)
                dve.wait_ge(eb_step, 3)
                v.tensor_tensor(eb_rest[:, 1, :], eb_rest[:, 0, :], eb_part[:, 1, :], ALU.subtract).then_inc(eb_step, 1)
                dve.wait_ge(eb_step, 4)
                v.tensor_copy(eb_part[:, 2, :], eb_rest[:, 1, :]).then_inc(eb_step, 1)

            def expert_lo(e):
                dve.wait_ge(ew_hi_ready, e + 1)
                v.tensor_tensor(ew_lo[:, :, e, :], E[e % 2][:, :].rearrange("p (k c) -> p k c", k=KC),
                                ew_hi[:, :, e, :].bitcast(F32), ALU.subtract).then_inc(ew_lo_ready, 1)

            def ln_stats(src, st, mv, step, n):
                for s in range(2):
                    last = v.bn_stats(st[:, s, :], src[:, s, :])
                last.then_inc(step, 1)
                wait_alone(dve, step, n + 1)
                for s in range(2):
                    last = v.bn_aggr(mv[:, s, :], st[:, s, :])
                last.then_inc(step, 1)

            def row_max(p, u):
                dve.wait_ge(s_done, 8 * p + u + 1)
                wait_alone(dve, exp_ready, 8 * p + u - 1)
                for j in range(4):
                    last = v.tensor_tensor_reduce(neg_s[:, u % 2, j, :], S[u % 2][:, j * P:(j + 1) * P], causal,
                                                  -1.0, 3.4e38, ALU.add, ALU.min,
                                                  accum_out=neg_max[:, u, j:j + 1])
                last.then_inc(max_ready, 1)

            def exp_lo(p, u):
                dve.wait_ge(eh_ready, 8 * p + u + 1)
                v.tensor_tensor(e_lo[:, u % 2, :, :], TB[:, :].rearrange("p (j t) -> p j t", j=4),
                                e_hi[:, u % 2, :, :], ALU.subtract).then_inc(el_ready, 1)
                if isinstance(p, int) and p == 0:
                    if u >= 1:
                        expert_lo(u - 1)
                    if u == 7:
                        expert_lo(u)

            def normalise(p, u):
                n = 4 * p + u // 2
                s, half = u // 4, u % 4 // 2
                dve.wait_ge(pv_done, 8 * p + u + 1)
                if u == 1:
                    wait(dve, ot_done, p)
                ob = OB[:, 0:8 * VC].rearrange("p (h c) -> p h c", c=VC)
                v.reciprocal(inv_sum[:].rearrange("p a h -> p (a h)"), ob[:, :, VC - 1])
                v.tensor_reduce(o_sum[:].rearrange("p a h d -> p (a h) d"), ob[:, :, 0:VC - 1].rearrange("p h (k d) -> p h d k", k=3), AX_X,
                                ALU.add).then_inc(norm_step, 1)
                dve.wait_ge(norm_step, n + 1)
                v.tensor_tensor(o_n[:, s, :, half, :, :], o_sum[:],
                                inv_sum[:].unsqueeze(3).broadcast_to([P, 2, 4, HD]), ALU.mult
                                ).then_inc(norm_ready, 1)

            def accumulate(p, f):
                dve.wait_ge(silu_ready, 8 * p + 2 * f + 2)
                if f == 0:
                    wait(dve, mt_done, p)
                for j in range(2):
                    for s in range(2):
                        n = 16 * p + 4 * f + 2 * j + s
                        w = w_tok[:, s, 2 * f + j:2 * f + j + 1]
                        term = act_e[:, (2 * f + s) % 4, j, :]
                        if f == 0 and j == 0:
                            ins = v.tensor_scalar(mix[:, s, :], term, w, None, ALU.mult)
                        else:
                            dve.wait_ge(acc_step, n - 1)
                            ins = v.scalar_tensor_tensor(out=mix[:, s, :], in0=term, scalar=w,
                                                         in1=mix[:, s, :], op0=ALU.mult, op1=ALU.add)
                        ins.then_inc(acc_step, 1)

            def attention_lo(p):
                lo_of(G0, oT_hi, oT_lo, oTh_ready, p + 1, oTl_ready)

            def mixture_lo(p):
                lo_of(G1, mT_hi, mT_lo, mTh_ready, p + 1, mTl_ready)

            def context_lo(p):
                lo_of(G0, cT_hi, cT_lo, cTh_ready, p + 1, cTl_ready)

            def xn_lo(p):
                lo_of(G0, xT_hi, xT_lo, xTh_ready, p + 1, xTl_ready)

            def xn2_lo(p):
                lo_of(G1, x2T_hi, x2T_lo, x2h_ready, p + 1, x2l_ready)

            def add_residual(p):
                dve.wait_ge(p_done, p + 1)
                dve.wait_ge(xb_ready, p + 1)
                wait(dve, x1_copied, p)
                v.tensor_tensor(x1[:, :, :], G0[:, :].rearrange("p (s c) -> p s c", s=2), xb[:],
                                ALU.add).then_inc(x1_ready, 1)

            def statistics_1(p):
                dve.wait_ge(x_loaded, 16 * p + 16)
                wait(dve, rs1_step, 3 * p)
                ln_stats(x_in, st1, mv1, ln1_step, 2 * p)

            def statistics_2(p):
                dve.wait_ge(x1_ready, p + 1)
                wait(dve, rs2_step, 3 * p)
                ln_stats(x1, st2, mv2, ln2_step, 2 * p)

            def finish(p):
                dve.wait_ge(comb_done, p + 1)
                dve.wait_ge(x1_copied, p + 1)
                wait(dve, y_stored, 16 * p)
                v.tensor_tensor(y[:, :, :], G1[:, :].rearrange("p (s c) -> p s c", s=2), x1_kept[:],
                                ALU.add).then_inc(y_ready, 1)

            def router_max(p):
                dve.wait_ge(gt_done, p + 1)
                lg = G1[:, 0:256].rearrange("p (s t) -> p s t", s=2)[:, :, 0:NE]
                v.tensor_reduce(r_max[:], lg, AX_X, ALU.max, negate=True).then_inc(rmax_ready, 1)
                dve.wait_ge(rmax_ready, p + 1)
                v.tensor_tensor(r_sub[:], lg, r_max[:].unsqueeze(2).broadcast_to([P, 2, NE]), ALU.add
                                ).then_inc(rsub_ready, 1)

            def router_compare(p):
                dve.wait_ge(rexp_ready, p + 1)
                v.tensor_reduce(r_sum[:], r_exp[:], AX_X, ALU.add).then_inc(prob_step, 1)
                dve.wait_ge(prob_step, 3 * p + 1)
                v.reciprocal(r_inv[:], r_sum[:]).then_inc(prob_step, 1)
                dve.wait_ge(prob_step, 3 * p + 2)
                v.tensor_tensor(prob[:], r_exp[:], r_inv[:].unsqueeze(2).broadcast_to([P, 2, NE]),
                                ALU.mult).then_inc(prob_step, 1)
                dve.wait_ge(prob_step, 3 * p + 3)
                of_j = prob[:].unsqueeze(2).broadcast_to([P, 2, NE, NE])
                of_e = prob[:].unsqueeze(3).broadcast_to([P, 2, NE, NE])
                v.tensor_tensor(cmp_gt[:], of_j, of_e, ALU.is_gt)
                v.tensor_tensor(cmp_eq[:], of_j, of_e, ALU.is_equal).then_inc(cmp_ready, 1)

            def router_weights(p):
                dve.wait_ge(cmp_step, 2 * p + 2)
                v.tensor_reduce(rank[:], cmp_gt[:], AX_X, ALU.add).then_inc(rank_step, 1)
                dve.wait_ge(rank_step, 2 * p + 1)
                v.scalar_tensor_tensor(out=w_tok[:], in0=rank[:], scalar=1.5, in1=prob[:],
                                       op0=ALU.is_lt, op1=ALU.mult).then_inc(rank_step, 1)
                dve.wait_ge(rank_step, 2 * p + 2)

            def step(i):
                p0, p1, p2, p3, p4, on = stages(i)
                if on[2]:
                    row_max(p2, 0)
                if on[4]:
                    accumulate(p4, 3)
                if on[3]:
                    add_residual(p3)
                if on[2]:
                    row_max(p2, 1)
                    row_max(p2, 2)
                if on[1]:
                    context_lo(p1)
                if on[4]:
                    mixture_lo(p4)
                if on[2]:
                    exp_lo(p2, 0)
                    row_max(p2, 3)
                if on[3]:
                    statistics_2(p3)
                if on[2]:
                    exp_lo(p2, 1)
                    row_max(p2, 4)
                if on[1]:
                    xn_lo(p1)
                if on[4]:
                    finish(p4)
                if on[2]:
                    row_max(p2, 5)
                    exp_lo(p2, 2)
                    normalise(p2, 1)
                    row_max(p2, 6)
                    exp_lo(p2, 3)
                if on[3]:
                    xn2_lo(p3)
                if on[2]:
                    row_max(p2, 7)
                    exp_lo(p2, 4)
                if on[0]:
                    statistics_1(p0)
                if on[3]:
                    router_max(p3)
                if on[2]:
                    normalise(p2, 3)
                    exp_lo(p2, 5)
                if on[3]:
                    router_compare(p3)
                    router_weights(p3)
                if on[2]:
                    exp_lo(p2, 6)
                    normalise(p2, 5)
                if on[3]:
                    accumulate(p3, 0)
                if on[2]:
                    exp_lo(p2, 7)
                if on[3]:
                    accumulate(p3, 1)
                if on[2]:
                    normalise(p2, 7)
                if on[3]:
                    accumulate(p3, 2)
                if on[2]:
                    attention_lo(p2)
                if isinstance(i, int) and i == 1:
                    split_expert_bias()

            step(0)
            prepare_weights()
            run_steps(dve, step)

        @block.gpsimd
        def _(pool):
            g = nc.gpsimd
            g.memset(half_neg[:], -0.5)
            g.memset(bias_sel[:], 0.0).then_inc(pool_setup, 1)
            g.memset(ebias[:], 0.0).then_inc(pool_setup, 1)
            pool.wait_ge(pool_setup, 2)
            g.memset(bias_sel[0:3, :], 1.0).then_inc(pool_setup, 1)

            def heads(t):
                return t.rearrange("p s (h d) -> p s h d", d=HD)

            def round_to(dst, src):
                return g.tensor_scalar(dst, src, 1.0, 1.0, ALU.mult, ALU.mult)

            def inverse_deviation(rs, ve, mv, step, n):
                g.tensor_scalar(ve[:, 0, :], mv[:, :, 1], 1.0, EPS, ALU.mult, ALU.add)
                g.tensor_scalar(ve[:, 1, :], mv[:, :, 0], -1.0, 1.0, ALU.mult, ALU.mult).then_inc(step, 1)
                pool.wait_ge(step, n + 1)
                g.tensor_tensor(rs[:, 0, :], ve[:, 0, :], half_neg[:], ALU.pow).then_inc(step, 1)
                pool.wait_ge(step, n + 2)
                g.tensor_tensor(rs[:, 1, :], rs[:, 0, :], ve[:, 1, :], ALU.mult).then_inc(step, 1)

            def bias_residual(p):
                pool.wait_ge(res_loaded, 16 * p + 16)
                wait(pool, x1_ready, p)
                g.tensor_tensor(xb[:], x_res[:], bo_row[:].unsqueeze(1).broadcast_to([P, 2, C]), ALU.add
                                ).then_inc(xb_ready, 1)

            def deviation_1(p):
                pool.wait_ge(ln1_step, 2 * p + 2)
                wait_alone(pool, xn_ready, p)
                inverse_deviation(rs1, ve1, mv1, rs1_step, 3 * p)

            def deviation_2(p):
                pool.wait_ge(ln2_step, 2 * p + 2)
                wait_alone(pool, xn2_ready, p)
                inverse_deviation(rs2, ve2, mv2, rs2_step, 3 * p)

            def keep_x1(p):
                pool.wait_ge(xn2_ready, p + 1)
                wait_alone(pool, y_ready, p)
                g.tensor_scalar(x1_kept[:], x1[:], 1.0, 1.0, ALU.mult, ALU.mult).then_inc(x1_copied, 1)

            def round_keys(p):
                wait_alone(pool, k32_ready, p + 1)
                round_to(k_round[:], k32[:]).then_inc(k_rounded, 1)
                pool.wait_ge(k_rounded, 2 * p + 1)
                g.tensor_tensor(k_rest[:], k32[:], k_round[:].bitcast(F32), ALU.subtract).then_inc(k_rounded, 1)

            def split_keys(p):
                pool.wait_ge(k_rounded, 2 * p + 2)
                wait_alone(pool, s_done, 8 * p)
                for dst, src in ((k_hi, k_round[:].bitcast(F32)), (k_lo, k_rest[:])):
                    for r in range(2):
                        for k in range(KC):
                            last = g.tensor_scalar(dst[:, k, :, r, :],
                                                   src[:, k, :].rearrange("p (s t) -> p s t", s=2),
                                                   parity[r], 1.0, ALU.mult, ALU.mult)
                last.then_inc(k_split, 1)

            def split_queries(p):
                pool.wait_ge(q32_ready, p + 1)
                wait_alone(pool, s_done, 8 * p)
                q_in = q32[:, :, :].rearrange("p a (s t) -> p a s t", s=2)
                round_to(q_hi[:, :, :, :], q_in).then_inc(q_split, 1)
                pool.wait_ge(q_split, 2 * p + 1)
                g.tensor_tensor(q_lo[:, :, :, :], q_in, q_hi[:, :, :, :].bitcast(F32), ALU.subtract
                                ).then_inc(q_split, 1)

            def split_values(p):
                n = 6 * p
                pool.wait_ge(v_raw_ready, p + 1)
                g.tensor_tensor(v32[:], v_raw[:], bv_row[:].unsqueeze(1).broadcast_to([P, 2, C]), ALU.add
                                ).then_inc(v_split, 1)
                pool.wait_ge(v_split, n + 1)
                wait_alone(pool, pv_done, 8 * p)
                round_to(v_part[:, :, :, 0:HD], heads(v32[:])).then_inc(v_split, 1)
                pool.wait_ge(v_split, n + 2)
                g.tensor_tensor(heads(v_rest[:]), heads(v32[:]), v_part[:, :, :, 0:HD], ALU.subtract
                                ).then_inc(v_split, 1)
                wait_alone(pool, v_split, n + 3)
                round_to(v_part[:, :, :, HD:2 * HD], heads(v_rest[:])).then_inc(v_split, 1)
                pool.wait_ge(v_split, n + 4)
                g.tensor_tensor(heads(v_rest[:]), heads(v_rest[:]), v_part[:, :, :, HD:2 * HD], ALU.subtract
                                ).then_inc(v_split, 1)
                wait_alone(pool, v_split, n + 5)
                round_to(v_part[:, :, :, 2 * HD:3 * HD], heads(v_rest[:])).then_inc(v_split, 1)

            def count_before(p):
                pool.wait_ge(cmp_ready, p + 1)
                low = cst[:, C_LOWER:C_LOWER + 64].rearrange("p (e j) -> p e j", e=NE).unsqueeze(1)
                g.tensor_tensor(cmp_eq[:], cmp_eq[:], low.broadcast_to([P, 2, NE, NE]), ALU.mult
                                ).then_inc(cmp_step, 1)
                pool.wait_ge(cmp_step, 2 * p + 1)
                g.tensor_tensor(cmp_gt[:], cmp_gt[:], cmp_eq[:], ALU.add).then_inc(cmp_step, 1)

            def step(i):
                p0, p1, p2, p3, p4, on = stages(i)
                if on[1]:
                    round_keys(p1)
                if on[3]:
                    deviation_2(p3)
                if on[1]:
                    split_keys(p1)
                    split_queries(p1)
                if on[2]:
                    bias_residual(p2)
                if on[0]:
                    deviation_1(p0)
                if on[3]:
                    count_before(p3)
                    keep_x1(p3)
                if on[1]:
                    split_values(p1)

            step(0)
            pool.wait_ge(consts_ready, 2)
            run_steps(pool, step)


_INS = ['x', 'ctx_1024', 'g_xattn', 'g_ffn', 'L0_xattn_wq', 'L0_xattn_bq', 'L0_xattn_wk', 'L0_xattn_bk',
        'L0_xattn_wv', 'L0_xattn_bv', 'L0_xattn_wo', 'L0_xattn_bo', 'L0_ffn_gate_w', 'L0_ffn_expert_w',
        'L0_ffn_expert_b', 'L0_ffn_combine_w']
_OUTS = [((64, 128, 256), 'float32')]


def kernel(**inputs):
    import numpy as _np
    import concourse.bacc as _bacc
    from concourse import mybir as _mybir
    from concourse.bass_utils import run_bass_kernel_spmd as _run

    nc = _bacc.Bacc("TRN2", target_bir_lowering=False, num_devices=1)
    arrays, args = {}, []
    for name in _INS:
        a = _np.ascontiguousarray(inputs[name])
        arrays[f"in_{name}_dram"] = a
        args.append(nc.dram_tensor(f"in_{name}_dram", a.shape, _mybir.dt.from_np(a.dtype), kind="ExternalInput").ap())
    c = _np.zeros((P, C_COLS), _np.float32)
    c[:, C_IDENT:C_IDENT + P] = _np.eye(P)
    c[:, C_CAUSAL:C_CAUSAL + P] = _np.triu(_np.full((P, P), -3.0e38), 1)
    c[:, C_PARITY] = _np.arange(P) // 16 % 2 == 0
    c[:, C_PARITY + 1] = _np.arange(P) // 16 % 2 == 1
    c[:, C_LOWER:C_LOWER + 64] = _np.tril(_np.ones((8, 8)), -1).reshape(1, 64)
    arrays["consts_dram"] = c
    args.append(nc.dram_tensor("consts_dram", c.shape, _mybir.dt.float32, kind="ExternalInput").ap())
    for i, (shape, dtype) in enumerate(_OUTS):
        dt = _mybir.dt.from_np(_np.dtype(dtype))
        args.append(nc.dram_tensor(f"out_{i}_dram", shape, dt, kind="ExternalOutput").ap())
    flamingo_block(nc, *args)
    r = _run(nc, [arrays], core_ids=[0])
    got = tuple(r.results[0][f"out_{i}_dram"] for i in range(len(_OUTS)))
    return got[0]
```
